# Optimizing a Trainium2 kernel written in Bass

```python
import numpy as np
import jax
import jax.numpy as jnp

def _softmax(x, axis=-1):
    return jax.nn.softmax(x, axis=axis)
def _gelu(x):
    return jax.nn.gelu(x, approximate=True)
def _silu(x):
    return jax.nn.silu(x)
def _sigmoid(x):
    return jax.nn.sigmoid(x)
def _layernorm(x, axis=-1, eps=1e-5):
    m = jnp.mean(x, axis=axis, keepdims=True)
    v = jnp.var(x, axis=axis, keepdims=True)
    return (x - m) / jnp.sqrt(v + eps)
def _scatter_add(tgt, idx, src, axis=0):
    return tgt.at[idx].add(src)
def _segment_sum(src, seg, n):
    return jax.ops.segment_sum(src, seg, n)

kernel_name = 'mk_conv_preact_d1_conv_nchw512_015b0d'

def setup_inputs(seed: int = 0):
    np.random.seed(seed)
    _w = jnp.asarray
    def _rec_inputs():
        import jax
        import jax.numpy as jnp
        _gk = jax.random.key(seed)
        x = -0.0001732 + 1 * jax.random.normal(jax.random.fold_in(_gk, 1), (4, 512, 48, 48), jnp.float32)
        return x
    x = _rec_inputs()
    def _L0_conv_setup():
        import jax, jax.numpy as jnp
        import numpy as np
        HEADS = 8
        key = jax.random.key(seed)
        ks = jax.random.split(key, 6)
        b, c, w, h = (4, 512, 48, 48)
        qc, vc = (512, 512)
        s = 1.0 / np.sqrt(c)
        return {'x': jax.random.normal(ks[0], (b, c, w, h), dtype=jnp.float32), 'Wq': jax.random.normal(ks[1], (qc, c), dtype=jnp.float32) * s, 'Wk': jax.random.normal(ks[2], (qc, c), dtype=jnp.float32) * s, 'Wv': jax.random.normal(ks[3], (vc, c), dtype=jnp.float32) * s, 'Wsc': jax.random.normal(ks[4], (vc, c), dtype=jnp.float32) * s, 'gamma': jax.random.normal(ks[5], (1, vc, 1, 1), dtype=jnp.float32)}
    _L0_conv_all = _L0_conv_setup()
    _L0_conv_in = {k: v for k, v in _L0_conv_all.items() if k in ('Wq', 'Wk', 'Wv', 'Wsc', 'gamma', )}
    del _L0_conv_all

    return {
        "x": x,
        "L0_conv_Wq": _L0_conv_in["Wq"],
        "L0_conv_Wk": _L0_conv_in["Wk"],
        "L0_conv_Wv": _L0_conv_in["Wv"],
        "L0_conv_Wsc": _L0_conv_in["Wsc"],
        "L0_conv_gamma": _L0_conv_in["gamma"],
    }

def reference(x, L0_conv_Wq, L0_conv_Wk, L0_conv_Wv, L0_conv_Wsc, L0_conv_gamma):
    import jax
    import jax.numpy as jnp
    def _L0_conv_ref(x, Wq, Wk, Wv, Wsc, gamma):
        import jax, jax.numpy as jnp
        import numpy as np
        HEADS = 8
        b, c, w, h = x.shape
        n = w * h
        dq = Wq.shape[0] // HEADS
        dv = Wv.shape[0] // HEADS
        q = jnp.einsum('bchw,oc->bohw', x, Wq).reshape(b, HEADS, dq, n)
        k = jnp.einsum('bchw,oc->bohw', x, Wk).reshape(b, HEADS, dq, n)
        v = jnp.einsum('bchw,oc->bohw', x, Wv).reshape(b, HEADS, dv, n)
        attn = jax.nn.softmax(jnp.einsum('bhdn,bhdm->bhnm', q, k), axis=-1)
        out = jnp.einsum('bhnm,bhdm->bnhd', attn, v)
        out = out.reshape(b, w, h, HEADS * dv).transpose(0, 3, 1, 2)
        sc = jnp.einsum('bchw,oc->bohw', x, Wsc)
        return gamma * out + sc

    def _gn(v, G=32, eps=1e-5):
        B_, C_, H_, W_ = v.shape
        g = v.reshape(B_, G, C_ // G, H_, W_)
        m = jnp.mean(g, axis=(2, 3, 4), keepdims=True)
        s = jnp.var(g, axis=(2, 3, 4), keepdims=True)
        return ((g - m) / jnp.sqrt(s + eps)).reshape(v.shape)

    def _ln_c(v, eps=1e-6):
        m = jnp.mean(v, axis=1, keepdims=True)
        s = jnp.var(v, axis=1, keepdims=True)
        return (v - m) / jnp.sqrt(s + eps)

    def _ln_t(v, eps=1e-5):
        m = jnp.mean(v, axis=-1, keepdims=True)
        s = jnp.var(v, axis=-1, keepdims=True)
        return (v - m) / jnp.sqrt(s + eps)

    def _to_tokens(v):
        B_, C_, H_, W_ = v.shape
        return v.reshape(B_, C_, H_ * W_).transpose(0, 2, 1)
    def _from_tokens(t, like):
        B_, C_, H_, W_ = like.shape
        return t.transpose(0, 2, 1).reshape(B_, C_, H_, W_)

    x = x + _L0_conv_ref(_gn(x), L0_conv_Wq, L0_conv_Wk, L0_conv_Wv, L0_conv_Wsc, L0_conv_gamma)
    return x


_drawn_inputs = setup_inputs


def setup_inputs(seed=0):
    import zlib

    import numpy as np

    out = dict(_drawn_inputs(seed))
    spreads = {}
    factors = {}
    for name, (base, spread) in spreads.items():
        noise = np.random.default_rng([zlib.crc32(name.encode()), seed]).standard_normal(out[name].shape)
        drawn = base * np.exp(spread * noise) if base else spread * noise
        out[name] = jnp.asarray(drawn.astype(out[name].dtype))
    for name, factor in factors.items():
        out[name] = (out[name] * factor).astype(out[name].dtype)
    return out
```

```python
from contextlib import ExitStack

import concourse.bass as bass
from concourse import mybir

F32 = mybir.dt.float32
F16 = mybir.dt.float16
BF16 = mybir.dt.bfloat16
ALU = mybir.AluOpType
ACT = mybir.ActivationFunctionType
AX = mybir.AxisListType

P = 128
BATCH, C, N = 4, 512, 48 * 48
HEADS = 8
D = C // HEADS
CT = C // P
BLOCKS = HEADS // 2
CH = 384
NCH = N // CH
QT = CH // P
MT = N // P
V1 = 2 * D + 1
OW = V1 + 1
PB = 3
PAIR = 2 * CH
PARTS = N // PAIR
GROUP = C // 32
EPS = 1e-5
WS = 64.0
QS = 8.0
ONE = 256.0
SS = QS * QS
UNITS = NCH * MT

U_W, U_GN, U_SC, U_V, U_QK, U_SHIFT, U_FIN = 4 * CT, 2, CT * 3, MT, NCH, 1, 3


def build(nc, x, wq, wk, wv, wsc, gamma, out):
    ctx = ExitStack()
    with ctx:
        def sb(name, shape, dt):
            return ctx.enter_context(nc.sbuf_tensor(name, shape, dt))

        def sem(name):
            return ctx.enter_context(nc.semaphore(name))

        QH = sb("QH", [P, 2, 2, N], F16)
        KH = sb("KH", [P, 2, 2, N], F16)
        QB = sb("QB", [P, 2, 2, N], F16)
        KB = sb("KB", [P, 2, 2, N], F16)
        V = sb("V", [P, MT, HEADS * V1], F16)
        xh = sb("xh", [P, CT, N], F16)
        xl = sb("xl", [P, CT, N], F16)
        WT = sb("WT", [P, 4, 2, CT, C], F16)
        PE32 = sb("PE32", [P, PB, PAIR], F32)
        PLO = sb("PLO", [P, PB, PAIR], F16)
        xr = sb("xr", [P, N], F32)
        attn = sb("attn", [P, N], F32)
        Oe = sb("Oe", [P, 2, QT, V1], F32)
        gam = sb("gam", [P, C], F32)
        identf = sb("identf", [P, P], F32)
        identh = sb("identh", [P, P], F16)
        gmat = sb("gmat", [P, P], F32)
        mx3 = sb("mx3", [P, 2, MT * PARTS], F32)
        cmx = sb("cmx", [P, 2 * MT], F32)
        cneg = sb("cneg", [P, 2 * MT], F32)
        c16 = sb("c16", [P, 4 * MT], F16)
        cT = sb("cT", [4 * MT, P], F16)
        rc = sb("rc", [P, 2, QT, 1], F32)
        stat = sb("stat", [P, CT, NCH, 6], F32)
        mv = sb("mv", [P, CT, 2], F32)
        gn = sb("gn", [P, 10, CT], F32)
        gn_mean, gn_dev, gn_sq, gn_var, gn_ve, gn_root, gn_r, gn_a, gn_b, gn_rstd = (
            gn[:, i, :] for i in range(10))

        SL = [ctx.enter_context(nc.psum_tensor(f"SL{i}", [P, 2, 512], F32)) for i in range(2)]
        MX = ctx.enter_context(nc.psum_tensor("MX", [P, 2, 512], F32))
        OB = ctx.enter_context(nc.psum_tensor("OB", [P, 2, 512], F32))

        stage = PE32[:, :, :].rearrange("p a n -> p (a n)")[:, 0:2 * PAIR].bitcast(F16).rearrange(
            "p (s a n) -> p s a n", s=2, a=4)
        wnat = [t[:, :, :].rearrange("p t n -> p (t n)").bitcast(F32) for t in (xh, xl)]
        xrc = xr[:, :].rearrange("p (s n) -> p s n", s=3)

        s_const = sem("s_const")
        s_wld = sem("s_wld")
        s_gam = sem("s_gam")
        s_d = sem("s_d")
        s_hi = sem("s_hi")
        s_dfree = sem("s_dfree")
        s_score = sem("s_score")
        s_exp = sem("s_exp")
        s_rest = sem("s_rest")
        s_restp = sem("s_restp")
        s_pfree = sem("s_pfree")
        s_mx = sem("s_mx")
        s_mxf = sem("s_mxf")
        s_oe = sem("s_oe")
        s_rc = sem("s_rc")
        s_pool = sem("s_pool")
        s_post = sem("s_post")
        s_cc = sem("s_cc")
        s_ct = sem("s_ct")
        s_crow = sem("s_crow")
        s_pack = [sem(f"s_pack{i}") for i in range(2)]
        s_qk = sem("s_qk")
        s_gx = [sem(f"s_gx{i}") for i in range(2)]
        s_gd = sem("s_gd")
        s_gt = sem("s_gt")
        s_gh = sem("s_gh")
        s_gv = sem("s_gv")
        s_mark = sem("s_mark")
        s_phase = sem("s_phase")
        s_gn0 = sem("s_gn0")
        s_gn = sem("s_gn")
        s_gs = sem("s_gs")
        s_ld = [sem(f"s_ld{i}") for i in range(3)]
        s_add = sem("s_add")
        s_st = [sem(f"s_st{i}") for i in range(3)]

        block = ctx.enter_context(nc.Block())

        class At:

            def __init__(self):
                self.d = self.hi = self.blk = self.gn = self.ring = self.qk = self.mxblk = 0

            def goto_body(self, b):
                self.d = self.d + b * (U_GN + U_SC + U_V + BLOCKS * (U_QK + U_SHIFT + U_FIN))
                self.hi = self.hi + b * (U_V + BLOCKS * U_QK)
                self.blk = self.blk + b * BLOCKS
                self.gn = self.gn + b
                self.ring = self.ring + b * (BLOCKS + 4)
                self.qk = self.qk + b * BLOCKS
                self.mxblk = self.mxblk + b * BLOCKS
                return self

        def program(eng, do):
            at = At()
            do.weights(at)
            do.norm(at, 0)
            do.shortcut(at, 0)
            do.values(at)
            do.qk(at, 0)
            do.maxima(at)
            do.shift(at, 0)
            do.qk(at, 1)

            def body(b, at, last):
                for j in range(BLOCKS):
                    following = not last or j + 1 < BLOCKS
                    do.attend(at, b, j, following)
                    if following:
                        do.shift(at, (j + 1) % 2)
                    do.finish(at, b, j)
                    if j == BLOCKS - 2 and not last:
                        do.norm(at, b + 1)
                        do.shortcut(at, b + 1)
                    if j == BLOCKS - 1 and not last:
                        do.values(at)
                    if not last or j + 2 < BLOCKS:
                        do.qk(at, (j + 2) % BLOCKS)

            def placed(b):
                a = At()
                a.d, a.hi, a.blk, a.gn = at.d, at.hi, at.blk, at.gn
                a.ring, a.qk, a.mxblk = at.ring, at.qk, at.mxblk
                return a.goto_body(b)

            with eng.Fori(0, BATCH - 1) as b:
                body(b, placed(b), False)
            body(BATCH - 1, placed(BATCH - 1), True)

        def attend_chunks(eng, chunk):
            chunk(0, True)
            with eng.Fori(1, NCH) as c:
                chunk(c, False)

        def exps_before(at):
            return at.blk * UNITS

        @block.sync
        def _(sp):
            class Do:
                def weights(self, at):
                    for i, w in enumerate((wq, wk, wv, wsc)):
                        dst = wnat[i // 2][:, (i % 2) * CT * C:(i % 2 + 1) * CT * C]
                        sp.dma_start(dst.rearrange("p (t c) -> p t c", t=CT),
                                     w.rearrange("(t p) c -> p t c", p=P)).then_inc(s_wld, 16)
                    sp.dma_start(gam[:, :], gamma.partition_broadcast(P)).then_inc(s_gam, 16)

                def norm(self, at, b):
                    sp.wait_ge(s_d, at.d)
                    if not isinstance(b, int):
                        for s in range(3):
                            sp.wait_ge(s_st[s], 16 * at.ring)
                    for n in range(2 * CT):
                        if n >= 2:
                            sp.wait_ge(s_gd, 2 * CT * at.gn + n - 1)
                        sp.dma_start((xr, attn)[n % 2][:, :],
                                     x[bass.ds(b * C + (n % CT) * P, P), :]).then_inc(s_gx[n % 2], 16)
                    at.gn += 1
                    at.d += U_GN

                def piece(self, at, n):
                    if isinstance(at.ring, int) and at.ring + n // 3 == 0:
                        return
                    sp.wait_ge(s_st[n % 3], 16 * (at.ring + n // 3))

                def shortcut(self, at, b):
                    def load(n):
                        self.piece(at, n)
                        sp.dma_start(xrc[:, n % 3, :], x[bass.ds(b * C + (n // 3) * P, P),
                                     (n % 3) * PAIR:(n % 3 + 1) * PAIR]).then_inc(s_ld[n % 3], 16)
                    sp.wait_ge(s_gd, 2 * CT * at.gn)
                    for n in range(3):
                        load(n)
                    for n in range(U_SC):
                        sp.wait_ge(s_add, 3 * at.ring + n + 1)
                        sp.dma_start(out[bass.ds(b * C + (n // 3) * P, P),
                                     (n % 3) * PAIR:(n % 3 + 1) * PAIR], xrc[:, n % 3, :]
                                     ).then_inc(s_st[n % 3], 16)
                        if n + 3 < U_SC:
                            load(n + 3)
                    at.ring += CT
                    at.d += U_SC

                def values(self, at):
                    at.d += U_V
                    at.hi += U_V

                def qk(self, at, j):
                    par = j % 2
                    with sp.Fori(0, NCH // 2) as a:
                        for u in range(2):
                            q0 = a * PAIR + u * CH
                            sp.wait_ge(s_qk, at.qk * NCH + a * 2 + u + 1)
                            for h in range(2):
                                hp = slice(h * D, (h + 1) * D)
                                for to, lane, part in ((QH, 0, 0), (QB, 0, 0), (KH, 0, 1), (KH, D, 1),
                                                       (QH, D, 2), (KB, 0, 3)):
                                    sp.dma_start(to[lane:lane + D, par, h, bass.ds(q0, CH)],
                                                 stage[hp, u, part, :]).then_inc(s_pack[u], 16)
                    at.qk += 1
                    at.d += U_QK
                    at.hi += U_QK

                def maxima(self, at):
                    at.mxblk += 1

                def shift(self, at, par):
                    sp.wait_ge(s_ct, at.mxblk)
                    for h in range(2):
                        for r in range(2):
                            row = (2 * r + h) * MT
                            sp.dma_start(QB[D + r:D + r + 1, par, h, :].rearrange("o (a n) -> o a n", n=P),
                                         cT[row:row + MT, :]).then_inc(s_crow, 16)
                    at.d += U_SHIFT

                def attend(self, at, b, j, following):
                    for n in range(3):
                        self.piece(at, n)
                        sp.dma_start(xrc[:, n, :], out[bass.ds(b * C + j * P, P), n * PAIR:(n + 1) * PAIR]
                                     ).then_inc(s_ld[n], 16)
                    at.blk += 1
                    at.mxblk += 1 if following else 0

                def finish(self, at, b, j):
                    for n in range(3):
                        sp.wait_ge(s_add, 3 * at.ring + n + 1)
                        sp.dma_start(out[bass.ds(b * C + j * P, P), n * PAIR:(n + 1) * PAIR],
                                     xrc[:, n, :]).then_inc(s_st[n], 16)
                    at.ring += 1
                    at.d += U_FIN

            program(sp, Do())
            for s in range(3):
                sp.wait_ge(s_st[s], 16 * BATCH * (CT + BLOCKS))

        @block.tensor
        def _(pe):
            def claim(at, exps=True):
                if exps and not (isinstance(at.blk, int) and at.blk == 0):
                    pe.wait_ge(s_exp, exps_before(at))
                pe.wait_ge(s_dfree, at.d)
                pe.sem_inc(s_phase, 1)

            def three(dst, terms):
                n = 0
                for lhs, rhs in terms:
                    last = pe.matmul(dst, lhs, rhs, start=n == 0, stop=n == len(terms) - 1)
                    n += 1
                return last

            PARTS3 = [(0, 0), (0, 1), (1, 0)]
            xp = (xh, xl)

            class Do:
                def weights(self, at):
                    pe.wait_ge(s_const, 5)
                    pe.wait_ge(s_wld, 64)
                    for w in range(4):
                        wn = wnat[w // 2][:, (w % 2) * CT * C:(w % 2 + 1) * CT * C].rearrange(
                            "p (t c) -> p t c", t=CT)
                        for t in range(CT):
                            n = w * CT + t
                            if n >= 2:
                                pe.wait_ge(s_dfree, n - 1)
                            for o in range(CT):
                                last = pe.transpose(SL[n % 2][:, 0, o * P:(o + 1) * P],
                                                    wn[:, o, t * P:(t + 1) * P], identf[:, :])
                            last.then_inc(s_d, 1)
                    at.d += U_W
                    at.hi += U_W

                def norm(self, at, b):
                    claim(at)
                    pe.wait_ge(s_gv, 3 * at.gn + 1)
                    pe.matmul(SL[0][:, 0, 0:CT], gmat[:, :], mv[:, :, 0], start=True, stop=True).then_inc(s_d, 1)
                    pe.wait_ge(s_gv, 3 * at.gn + 2)
                    pe.matmul(SL[1][:, 0, 0:CT], gmat[:, :], gn_var, start=True, stop=True).then_inc(s_d, 1)
                    at.gn += 1
                    at.d += U_GN

                def shortcut(self, at, b):
                    pe.wait_ge(s_gd, 2 * CT * at.gn)
                    claim(at)
                    with pe.Fori(0, CT // 2) as a:
                        for n in range(6):
                            pe.wait_ge(s_dfree, at.d + a * 6 + n - 1)
                            for u in range(2):
                                q0 = (n % 3) * PAIR + u * CH
                                last = three(SL[n % 2][:, u, 0:CH], [
                                    (WT[:, 3, wp, t, bass.ds(a * 2 * P + (n // 3) * P, P)],
                                     xp[p][:, t, q0:q0 + CH]) for t in range(CT) for wp, p in PARTS3])
                            last.then_inc(s_d, 1)
                    at.ring += CT
                    at.d += U_SC

                def values(self, at):
                    claim(at)
                    with pe.Fori(0, MT // 2) as a:
                        for u in range(2):
                            pe.wait_ge(s_dfree, at.d + a * 2 + u - 1)
                            three(SL[u][:, 0, :], [
                                (xp[p][:, t, bass.ds(a * 2 * P + u * P, P)], WT[:, 2, wp, t, :])
                                for t in range(CT) for wp, p in PARTS3]).then_inc(s_d, 1)
                    at.d += U_V
                    at.hi += U_V

                def qk(self, at, j):
                    claim(at)
                    with pe.Fori(0, NCH // 2) as a:
                        for u in range(2):
                            pe.wait_ge(s_dfree, at.d + a * 2 + u - 1)
                            for w in range(2):
                                last = three(SL[u][:, w, 0:CH], [
                                    (WT[:, w, wp, t, j * P:(j + 1) * P],
                                     xp[p][:, t, bass.ds(a * PAIR + u * CH, CH)])
                                    for t in range(CT) for wp, p in PARTS3])
                            last.then_inc(s_d, 1)
                    at.qk += 1
                    at.d += U_QK
                    at.hi += U_QK

                def top(self, dst, par, c, k):
                    i, h, t = k // (2 * PARTS), k // PARTS % 2, k % PARTS
                    for u in range(2):
                        k0 = t * PAIR + u * CH
                        last = pe.matmul(dst[:, u, 0:CH], QH[:, par, h, bass.ds(c * CH + i * P, P)],
                                         KH[:, par, h, k0:k0 + CH], start=True, stop=True)
                    last.then_inc(s_mx, 1)

                def maxima(self, at):
                    for u in range(2):
                        pe.wait_ge(s_pack[u], 12 * 16 * (NCH // 2) * at.qk)
                    claim(at)

                    def chunk(c, first):
                        for k in range(MT):
                            if not (first and k < 3):
                                pe.wait_ge(s_mxf, c * MT + k - 2)
                            self.top((MX, SL[0], SL[1])[k % 3], 0, c, k)

                    attend_chunks(pe, chunk)
                    pe.wait_ge(s_mxf, UNITS)
                    at.mxblk += 1

                def shift(self, at, par):
                    claim(at)
                    pe.wait_ge(s_cc, 3 * at.mxblk)
                    pe.transpose(SL[0][0:4 * MT, 0, :].bitcast(F16)[:, 0:P], c16[:, :], identh[:, :]
                                 ).then_inc(s_d, 1)
                    at.d += U_SHIFT

                def attend(self, at, b, j, following):
                    par = j % 2
                    for u in range(2):
                        pe.wait_ge(s_pack[u], 12 * 16 * (NCH // 2) * at.qk)
                    pe.wait_ge(s_crow, 64 * at.mxblk)
                    claim(at, exps=False)

                    def weigh(q, kk, first=False):
                        if kk % 3 < 2:
                            pe.wait_ge(s_rest, 12 * q + 2 * (kk // 3) + kk % 3 + 1)
                        else:
                            pe.wait_ge(s_restp, 12 * q + 2 * (kk // 3) + 2)
                        if kk == 0 and not first:
                            pe.wait_ge(s_oe, q)
                        for h in range(2):
                            v0 = (2 * j + h) * V1
                            for i in range(QT):
                                s0 = h * CH + i * P
                                acc = OB[:, h, i * OW:i * OW + V1]
                                upper = PE32[:, kk % PB, s0:s0 + P].bitcast(BF16)[:, 1:2 * P:2]
                                pe.matmul(acc, upper, V[:, kk, v0:v0 + V1], start=kk == 0 and i == 0,
                                          stop=False, skip_group_check=True)
                                last = pe.matmul(acc[:, D:V1], PLO[:, kk % PB, s0:s0 + P],
                                                 V[:, kk, v0 + D:v0 + V1], start=False,
                                                 stop=kk == MT - 1 and i == QT - 1, skip_group_check=True)
                        last.then_inc(s_pfree, 1)

                    def chunk(c, first):
                        q = at.blk * NCH + c
                        for k in range(MT):
                            if not (first and k < 2):
                                pe.wait_ge(s_exp, q * MT + k - 1)
                            for h in range(2):
                                pe.matmul(SL[k % 2][:, h, 0:CH], KH[:, par, h, k * P:(k + 1) * P],
                                          QH[:, par, h, bass.ds(c * CH, CH)], start=True, stop=False)
                                last = pe.matmul(SL[k % 2][:, h, 0:CH], KB[0:D + 2, par, h, k * P:(k + 1) * P],
                                                 QB[0:D + 2, par, h, bass.ds(c * CH, CH)],
                                                 start=False, stop=True)
                            last.then_inc(s_score, 1)
                            if following:
                                pe.wait_ge(s_mxf, (at.mxblk * NCH + c) * MT + k)
                                self.top(MX, 1 - par, c, k)
                            if k >= 2:
                                weigh(q, k - 2, first)
                            elif not first:
                                weigh(q - 1, MT + k - 2)

                    attend_chunks(pe, chunk)
                    for kk in (MT - 2, MT - 1):
                        weigh(at.blk * NCH + NCH - 1, kk)
                    at.blk += 1
                    at.mxblk += 1 if following else 0

                def finish(self, at, b, j):
                    claim(at)
                    pe.wait_ge(s_post, at.blk * NCH + 1)
                    for n in range(U_FIN):
                        if n >= 2:
                            pe.wait_ge(s_dfree, at.d + n - 1)
                        for u in range(2):
                            for i in range(QT):
                                t = (n * 2 + u) * QT + i
                                last = pe.transpose(SL[n % 2][:, u, i * P:(i + 1) * P],
                                                    attn[:, t * P:(t + 1) * P], identf[:, :])
                        last.then_inc(s_d, 1)
                    at.ring += 1
                    at.d += U_FIN

            program(pe, Do())

        @block.scalar
        def _(act):
            class Do:
                def weights(self, at):
                    for n in range(U_W):
                        act.wait_ge(s_d, n + 1)
                        act.activation(WT[:, n // CT, 0, n % CT, :], SL[n % 2][:, 0, :], ACT.Copy,
                                       scale=WS).then_inc(s_hi, 1)
                    at.d += U_W
                    at.hi += U_W

                def norm(self, at, b):
                    act.wait_ge(s_gv, 3 * at.gn + 3)
                    act.activation(gn_root, gn_ve, ACT.Sqrt).then_inc(s_gs, 1)
                    for t in range(CT):
                        act.wait_ge(s_gt, CT * at.gn + t + 1)
                        act.activation(xh[:, t, :], (xr, attn)[t % 2][:, :], ACT.Copy).then_inc(s_gh, 1)
                    at.gn += 1
                    at.d += U_GN

                def shortcut(self, at, b):
                    at.ring += CT
                    at.d += U_SC

                def values(self, at):
                    with act.Fori(0, MT // 2) as a:
                        for u in range(2):
                            act.wait_ge(s_d, at.d + a * 2 + u + 1)
                            vv = V[:, bass.ds(a * 2 + u, 1), :].rearrange("p a (h x) -> p (a h) x", x=V1)
                            act.activation(vv[:, :, D:2 * D],
                                           SL[u][:, 0, :].rearrange("p (h d) -> p h d", d=D),
                                           ACT.Copy, scale=QS / WS).then_inc(s_hi, 1)
                    at.d += U_V
                    at.hi += U_V

                def qk(self, at, j):
                    def chunks(a):
                        for u in range(2):
                            act.wait_ge(s_d, at.d + a * 2 + u + 1)
                            if not (isinstance(a, int) and isinstance(at.qk, int) and a + at.qk == 0):
                                act.wait_ge(s_pack[u], 12 * 16 * (NCH // 2 * at.qk + a))
                            act.activation(stage[:, u, 0:2, :], SL[u][:, :, 0:CH],
                                           ACT.Copy, scale=QS / WS).then_inc(s_hi, 1)

                    chunks(0)
                    with act.Fori(1, NCH // 2) as a:
                        chunks(a)
                    at.qk += 1
                    at.d += U_QK
                    at.hi += U_QK

                def maxima(self, at):
                    at.mxblk += 1

                def shift(self, at, par):
                    at.d += U_SHIFT

                def attend(self, at, b, j, following):
                    for u in range(2):
                        act.wait_ge(s_pack[u], 12 * 16 * (NCH // 2) * at.qk)

                    def evacuate(q):
                        act.wait_ge(s_pfree, (q + 1) * MT)
                        act.wait_ge(s_post, q + 1)
                        act.activation(Oe[:, :, :, :],
                                       OB[:, :, 0:QT * OW].rearrange("p h (i x) -> p h i x", x=OW)[:, :, :, 0:V1],
                                       ACT.Copy).then_inc(s_oe, 1)

                    def chunk(c, first):
                        q = at.blk * NCH + c
                        for k in range(MT):
                            if k == 2 and not first:
                                evacuate(q - 1)
                            act.wait_ge(s_score, q * MT + k + 1)
                            if not (first and k < PB):
                                act.wait_ge(s_pfree, q * MT + k - PB + 1)
                            act.activation(PE32[:, k % PB, :].rearrange("p (h n) -> p h n", h=2),
                                           SL[k % 2][:, :, 0:CH], ACT.Exp, scale=1.0 / SS).then_inc(s_exp, 1)

                    attend_chunks(act, chunk)
                    evacuate(at.blk * NCH + NCH - 1)
                    at.blk += 1
                    at.mxblk += 1 if following else 0

                def finish(self, at, b, j):
                    at.ring += 1
                    at.d += U_FIN

            program(act, Do())

        @block.vector
        def _(dve):
            class Do:
                def weights(self, at):
                    nc.vector.memset(gn[:, :, :], 0.0).then_inc(s_gn0, 1)
                    nc.vector.memset(KB[D:D + 2, :, :, :], ONE).then_inc(s_const, 1)
                    nc.vector.memset(V[:, :, :].rearrange("p a (h x) -> p (a h) x", x=V1)[:, :, 2 * D:V1],
                                     1.0).then_inc(s_const, 1)
                    for n in range(U_W):
                        dve.wait_ge(s_hi, n + 1)
                        nc.vector.scalar_tensor_tensor(
                            out=WT[:, n // CT, 1, n % CT, :], in0=SL[n % 2][:, 0, :], scalar=WS,
                            in1=WT[:, n // CT, 0, n % CT, :], op0=ALU.mult, op1=ALU.subtract
                            ).then_inc(s_dfree, 1)
                    dve.wait_ge(s_gam, 16)
                    dve.wait_ge(s_gn0, 1)
                    nc.vector.tensor_scalar(gam[:, :], gam[:, :], 1.0 / QS, None, ALU.mult).then_inc(s_const, 1)
                    at.d += U_W
                    at.hi += U_W

                def norm(self, at, b):
                    steps = [at.gn * 9]

                    def link(ins):
                        steps[0] = steps[0] + 1
                        ins.then_inc(s_gn, 1)
                        dve.wait_ge(s_gn, steps[0])

                    tiles = (xr, attn)
                    for t in range(CT):
                        dve.wait_ge(s_gx[t % 2], 16 * (CT * at.gn + t // 2 + 1))
                        for s in range(NCH):
                            last = nc.vector.bn_stats(stat[:, t, s, :], tiles[t % 2][:, s * CH:(s + 1) * CH])
                            if s == NCH - 1:
                                last.then_inc(s_gd, 1)
                    dve.wait_ge(s_gd, 2 * CT * at.gn + CT)
                    nc.vector.tensor_copy(gn_a, gn_b)
                    for t in range(CT):
                        aggr = nc.vector.bn_aggr(mv[:, t, :], stat[:, t, :, :].rearrange("p s x -> p (s x)"))
                    aggr.then_inc(s_gv, 1)
                    dve.wait_ge(s_d, at.d + 1)
                    link(nc.vector.tensor_copy(gn_mean, SL[0][:, 0, 0:CT]))
                    link(nc.vector.tensor_tensor(gn_dev, mv[:, :, 0], gn_mean, ALU.subtract))
                    link(nc.vector.tensor_tensor(gn_sq, gn_dev, gn_dev, ALU.mult))
                    nc.vector.tensor_tensor(gn_var, gn_sq, mv[:, :, 1], ALU.add).then_inc(s_gv, 1)
                    dve.wait_ge(s_d, at.d + 2)
                    nc.vector.tensor_scalar(gn_ve, SL[1][:, 0, 0:CT], EPS, None, ALU.add).then_inc(s_gv, 1)
                    dve.wait_ge(s_gs, at.gn + 1)
                    link(nc.vector.reciprocal(gn_r, gn_root))
                    link(nc.vector.tensor_tensor(gn_a, gn_r, gn_r, ALU.mult))
                    link(nc.vector.tensor_tensor(gn_b, gn_a, gn_ve, ALU.mult))
                    link(nc.vector.tensor_scalar(gn_a, gn_b, -0.5, 1.5, ALU.mult, ALU.add))
                    link(nc.vector.tensor_tensor(gn_rstd, gn_r, gn_a, ALU.mult))
                    link(nc.vector.tensor_copy(gn_b, gn_rstd))
                    nc.vector.tensor_copy(gn_a, gn_b).then_inc(s_dfree, 2)

                    def scale(t):
                        dve.wait_ge(s_gx[t % 2], 16 * (CT * at.gn + 2 + t // 2 + 1))
                        nc.vector.tensor_scalar(tiles[t % 2][:, :], tiles[t % 2][:, :], gn_mean[:, t:t + 1],
                                                gn_rstd[:, t:t + 1], ALU.subtract, ALU.mult).then_inc(s_gt, 1)

                    scale(0)
                    for t in range(CT):
                        if t + 1 < CT:
                            scale(t + 1)
                        dve.wait_ge(s_gh, CT * at.gn + t + 1)
                        nc.vector.tensor_tensor(xl[:, t, :], tiles[t % 2][:, :], xh[:, t, :],
                                                ALU.subtract).then_inc(s_gd, 1)
                    at.gn += 1
                    at.d += U_GN

                def shortcut(self, at, b):
                    with dve.Fori(0, CT // 2) as a:
                        for n in range(6):
                            dve.wait_ge(s_ld[n % 3], 16 * (at.ring + a * 2 + n // 3 + 1))
                            dve.wait_ge(s_d, at.d + a * 6 + n + 1)
                            piece = xrc[:, n % 3, :].rearrange("p (u n) -> p u n", u=2)
                            nc.vector.scalar_tensor_tensor(
                                out=piece, in0=SL[n % 2][:, :, 0:CH], scalar=1.0 / WS, in1=piece,
                                op0=ALU.mult, op1=ALU.add).then_inc(s_add, 1)
                            dve.wait_ge(s_add, 3 * at.ring + a * 6 + n + 1)
                            dve.sem_inc(s_dfree, 1)
                    at.ring += CT
                    at.d += U_SC

                def values(self, at):
                    with dve.Fori(0, MT // 2) as a:
                        for u in range(2):
                            dve.wait_ge(s_hi, at.hi + a * 2 + u + 1)
                            vv = V[:, bass.ds(a * 2 + u, 1), :].rearrange("p a (h x) -> p (a h) x", x=V1)
                            nc.vector.scalar_tensor_tensor(
                                out=vv[:, :, 0:D], in0=SL[u][:, 0, :].rearrange("p (h d) -> p h d", d=D),
                                scalar=QS / WS, in1=vv[:, :, D:2 * D], op0=ALU.mult, op1=ALU.subtract
                                ).then_inc(s_dfree, 1)
                    at.d += U_V
                    at.hi += U_V

                def qk(self, at, j):
                    with dve.Fori(0, NCH // 2) as a:
                        for u in range(2):
                            dve.wait_ge(s_hi, at.hi + a * 2 + u + 1)
                            nc.vector.scalar_tensor_tensor(
                                out=stage[:, u, 2:4, :], in0=SL[u][:, :, 0:CH], scalar=QS / WS,
                                in1=stage[:, u, 0:2, :], op0=ALU.mult, op1=ALU.subtract).then_inc(s_qk, 1)
                            dve.wait_ge(s_qk, at.qk * NCH + a * 2 + u + 1)
                            dve.sem_inc(s_dfree, 1)
                    at.qk += 1
                    at.d += U_QK
                    at.hi += U_QK

                def top(self, src, n, c, k):
                    i, h, t = k // (2 * PARTS), k // PARTS % 2, k % PARTS
                    dve.wait_ge(s_mx, n + k + 1)
                    nc.vector.tensor_reduce(mx3[:, h, bass.ds(c * QT * PARTS + i * PARTS + t, 1)],
                                            src[:, :, 0:CH], AX.XY, ALU.max).then_inc(s_mxf, 1)

                def maxima(self, at):
                    with dve.Fori(0, NCH) as c:
                        for k in range(MT):
                            self.top((MX, SL[0], SL[1])[k % 3], c * MT, c, k)
                    at.mxblk += 1

                def shift(self, at, par):
                    n = 3 * (at.mxblk - 1)
                    dve.wait_ge(s_mxf, at.mxblk * UNITS)
                    nc.vector.tensor_reduce(cmx[:, :], mx3[:, :, :].rearrange("p h (m t) -> p (h m) t", t=PARTS),
                                            AX.X, ALU.max).then_inc(s_cc, 1)
                    dve.wait_ge(s_cc, n + 1)
                    nc.vector.tensor_scalar(c16[:, 0:2 * MT], cmx[:, :], -1.0 / ONE, None, ALU.mult).then_inc(s_cc, 1)
                    dve.wait_ge(s_cc, n + 2)
                    nc.vector.scalar_tensor_tensor(out=c16[:, 2 * MT:], in0=cmx[:, :], scalar=-1.0 / ONE,
                                                   in1=c16[:, 0:2 * MT], op0=ALU.mult, op1=ALU.subtract
                                                   ).then_inc(s_cc, 1)
                    dve.wait_ge(s_d, at.d + 1)
                    if not (isinstance(at.mxblk, int) and at.mxblk == 1):
                        dve.wait_ge(s_crow, 64 * (at.mxblk - 1))
                    nc.vector.tensor_copy(cT[:, :], SL[0][0:4 * MT, 0, :].bitcast(F16)[:, 0:P]).then_inc(s_ct, 1)
                    dve.wait_ge(s_ct, at.mxblk)
                    dve.sem_inc(s_dfree, 1)
                    at.d += U_SHIFT

                def attend(self, at, b, j, following):
                    def chunk(c, first):
                        q = at.blk * NCH + c
                        for k in range(MT):
                            if following:
                                self.top(MX, (at.mxblk * NCH + c) * MT, c, k)
                            if k % 3 < 2:
                                dve.wait_ge(s_exp, q * MT + k + 1)
                                nc.vector.tensor_tensor(
                                    PLO[:, k % PB, :], PE32[:, k % PB, :],
                                    PE32[:, k % PB, :].bitcast(BF16)[:, 1:2 * PAIR:2],
                                    ALU.subtract).then_inc(s_rest, 1)
                            if k == 4 and not first:
                                invert(q - 1)

                    def invert(q):
                        dve.wait_ge(s_oe, q + 1)
                        nc.vector.reciprocal(rc[:, :, :, :], Oe[:, :, :, 2 * D:V1]).then_inc(s_rc, 1)

                    attend_chunks(dve, chunk)
                    invert(at.blk * NCH + NCH - 1)
                    at.blk += 1
                    at.mxblk += 1 if following else 0

                def finish(self, at, b, j):
                    for n in range(U_FIN):
                        dve.wait_ge(s_ld[n], 16 * (at.ring + 1))
                        dve.wait_ge(s_d, at.d + n + 1)
                        piece = xrc[:, n, :].rearrange("p (u n) -> p u n", u=2)
                        nc.vector.tensor_tensor(piece, SL[n % 2][:, :, 0:CH], piece, ALU.add).then_inc(s_add, 1)
                        dve.wait_ge(s_add, 3 * at.ring + n + 1)
                        dve.sem_inc(s_dfree, 1)
                    at.ring += 1
                    at.d += U_FIN

            program(dve, Do())

        @block.gpsimd
        def _(pool):
            class Do:
                def weights(self, at):
                    nc.gpsimd.memset(identf[:, :], 0.0).then_inc(s_pool, 1)
                    nc.gpsimd.memset(identh[:, :], 0.0).then_inc(s_pool, 1)
                    nc.gpsimd.memset(rc[:, :, :, :], 0.0).then_inc(s_post, 1)
                    nc.gpsimd.memset(gmat[:, :], 1.0 / GROUP).then_inc(s_pool, 1)
                    pool.wait_ge(s_pool, 3)
                    for m in (identf, identh):
                        nc.gpsimd.affine_select(out=m[:, :], in_=m[:, :], compare_op=ALU.not_equal, fill=1.0,
                                                base=0, pattern=[[-1, P]], channel_multiplier=1
                                                ).then_inc(s_const, 1)
                    g = gmat[:, :].rearrange("p (g i) -> p g i", i=GROUP)
                    nc.gpsimd.affine_select(out=g, in_=g, compare_op=ALU.is_ge, fill=0.0, base=0,
                                            pattern=[[-GROUP, P // GROUP], [0, GROUP]], channel_multiplier=1
                                            ).then_inc(s_pool, 1)
                    pool.wait_ge(s_pool, 4)
                    nc.gpsimd.affine_select(out=g, in_=g, compare_op=ALU.is_ge, fill=0.0, base=GROUP - 1,
                                            pattern=[[GROUP, P // GROUP], [0, GROUP]], channel_multiplier=-1
                                            ).then_inc(s_const, 1)
                    at.d += U_W
                    at.hi += U_W

                def norm(self, at, b):
                    at.gn += 1
                    at.d += U_GN

                def shortcut(self, at, b):
                    at.ring += CT
                    at.d += U_SC

                def values(self, at):
                    at.d += U_V
                    at.hi += U_V

                def qk(self, at, j):
                    at.qk += 1
                    at.d += U_QK
                    at.hi += U_QK

                def maxima(self, at):
                    at.mxblk += 1

                def shift(self, at, par):
                    at.d += U_SHIFT

                def attend(self, at, b, j, following):
                    pool.wait_ge(s_d, at.d)

                    def weigh_by(q, c):
                        step = 4 + 2 * q
                        sums = Oe[:, :, :, 0:D]
                        pool.wait_ge(s_oe, q + 1)
                        nc.gpsimd.tensor_tensor(sums, sums, Oe[:, :, :, D:2 * D], ALU.add).then_inc(s_pool, 1)
                        pool.wait_ge(s_rc, q + 1)
                        pool.wait_ge(s_pool, step + 1)
                        nc.gpsimd.tensor_tensor(sums, sums, rc[:, :, :, :].to_broadcast([P, 2, QT, D]),
                                                ALU.mult).then_inc(s_pool, 1)
                        pool.wait_ge(s_pool, step + 2)
                        pool.sem_inc(s_mark, 1)
                        g = gam[:, j * P:(j + 1) * P].rearrange("p (h o d) -> p h o d", h=2, o=1)
                        nc.gpsimd.tensor_tensor(
                            attn[:, bass.ds(c * CH, CH)].rearrange("p (i h d) -> p h i d", h=2, d=D),
                            sums, g.to_broadcast([P, 2, QT, D]), ALU.mult).then_inc(s_post, 1)

                    def chunk(c, first):
                        q = at.blk * NCH + c
                        for k in range(2, MT, 3):
                            pool.wait_ge(s_exp, q * MT + k + 1)
                            for h in range(2):
                                nc.gpsimd.tensor_tensor(
                                    PLO[:, k % PB, h * CH:(h + 1) * CH], PE32[:, k % PB, h * CH:(h + 1) * CH],
                                    PE32[:, k % PB, h * CH:(h + 1) * CH].bitcast(BF16)[:, 1:2 * CH:2],
                                    ALU.subtract).then_inc(s_restp, 1)
                            if k == 8 and not first:
                                weigh_by(q - 1, c - 1)

                    attend_chunks(pool, chunk)
                    weigh_by(at.blk * NCH + NCH - 1, NCH - 1)
                    at.blk += 1
                    at.mxblk += 1 if following else 0

                def finish(self, at, b, j):
                    at.ring += 1
                    at.d += U_FIN

            pool.wait_ge(s_gam, 16)
            program(pool, Do())


def kernel(x, L0_conv_Wq, L0_conv_Wk, L0_conv_Wv, L0_conv_Wsc, L0_conv_gamma):
    import numpy as np
    import concourse.bacc as bacc
    from concourse.bass_utils import run_bass_kernel_spmd

    nc = bacc.Bacc("TRN2", target_bir_lowering=False, num_devices=1, dynamic_dma_scratch_size=1024)
    arrays = {
        "x": np.ascontiguousarray(x).reshape(BATCH * C, N),
        "wq": np.ascontiguousarray(L0_conv_Wq),
        "wk": np.ascontiguousarray(L0_conv_Wk),
        "wv": np.ascontiguousarray(L0_conv_Wv),
        "wsc": np.ascontiguousarray(L0_conv_Wsc),
        "gamma": np.ascontiguousarray(L0_conv_gamma).reshape(C),
    }
    args = [nc.dram_tensor(k, a.shape, F32, kind="ExternalInput").ap() for k, a in arrays.items()]
    out = nc.dram_tensor("out", (BATCH * C, N), F32, kind="ExternalOutput").ap()
    build(nc, *args, out)
    r = run_bass_kernel_spmd(nc, [arrays], core_ids=[0])
    return r.results[0]["out"].reshape(np.shape(x))
```

```python
from contextlib import ExitStack

import concourse.bass as bass
from concourse import mybir

F32 = mybir.dt.float32
F16 = mybir.dt.float16
BF16 = mybir.dt.bfloat16
ALU = mybir.AluOpType
ACT = mybir.ActivationFunctionType
AX = mybir.AxisListType

P = 128
BATCH, C, N = 4, 512, 48 * 48
HEADS = 8
D = C // HEADS
CT = C // P
BLOCKS = HEADS // 2
CH = 384
NCH = N // CH
QT = CH // P
MT = N // P
V1 = 2 * D + 1
OW = V1 + 1
PB = 3
PAIR = 2 * CH
PARTS = N // CH
GROUP = C // 32
EPS = 1e-5
WS = 64.0
QS = 8.0
ONE = 256.0
SS = QS * QS
UNITS = NCH * MT
TOPS = 2 * UNITS

PACK = 6 * 16
SHARE = 384
G4 = CT * CH

U_W, U_GN, U_SC, U_V, U_QK, U_FIN = 4 * CT, 2, CT * 3, MT, NCH, 3
OPEN_TOPS = (range(0, 7), range(7, 14), range(14, 21), range(21, 29), range(29, 36))
Q_PARTS = ((0, 1), (1, NCH // 2))


def build(nc, x, wq, wk, wv, wsc, gamma, out):
    ctx = ExitStack()
    with ctx:
        def sb(name, shape, dt):
            return ctx.enter_context(nc.sbuf_tensor(name, shape, dt))

        def sem(name):
            return ctx.enter_context(nc.semaphore(name))

        QK = sb("QK", [P, 2, 2, 4, N], F16)
        QH, KH, QB, KB = (QK[:, :, :, i, :] for i in range(4))
        V = sb("V", [P, MT, HEADS * V1], F16)
        xh = sb("xh", [P, CT, N], F16)
        xl = sb("xl", [P, CT, N], F16)
        WT = sb("WT", [P, 4, 2, CT, C], F16)
        PE32 = sb("PE32", [P, PB, PAIR], F32)
        PLO = sb("PLO", [P, PB, PAIR], F16)
        xr = sb("xr", [P, N], F32)
        gx = sb("gx", [P, CT, CH], F32)
        attn = sb("attn", [P, N], F32)
        Oe = sb("Oe", [P, 2, QT, V1], F32)
        gam = sb("gam", [P, C], F32)
        identf = sb("identf", [P, P], F32)
        identh = sb("identh", [P, P], F16)
        gmat = sb("gmat", [P, P], F32)
        mx3 = sb("mx3", [P, 2, MT * PARTS], F32)
        cmx = sb("cmx", [P, 2 * MT], F32)
        cneg = sb("cneg", [P, 2 * MT], F32)
        c16 = sb("c16", [P, 4 * MT], F16)
        cT = sb("cT", [4 * MT, P], F16)
        rc = sb("rc", [P, 2, QT, 1], F32)
        stat = sb("stat", [P, CT, NCH * 6], F32)
        mv = sb("mv", [P, CT, 2], F32)
        gn = sb("gn", [P, 11, CT], F32)
        gn_mean, gn_dev, gn_sq, gn_var, gn_ve, gn_root, gn_r, gn_a, gn_b, gn_rstd, gn_bias = (
            gn[:, i, :] for i in range(11))

        SL = [ctx.enter_context(nc.psum_tensor(f"SL{i}", [P, 2, 512], F32)) for i in range(2)]
        MX = ctx.enter_context(nc.psum_tensor("MX", [P, 2, 512], F32))
        OB = ctx.enter_context(nc.psum_tensor("OB", [P, 2, 512], F32))

        stage = gx[:, :, :].rearrange("p t n -> p (t n)").bitcast(F16).rearrange(
            "p (s a n) -> p s a n", s=2, a=4)
        gx3 = (gx[:, :, :], *(t[:, 0:G4].rearrange("p (t n) -> p t n", t=CT) for t in (xr, attn)))
        wnat = [t[:, :, :].rearrange("p t n -> p (t n)").bitcast(F32) for t in (xh, xl)]
        xrc = xr[:, :].rearrange("p (s n) -> p s n", s=3)

        s_const = sem("s_const")
        s_wld = sem("s_wld")
        s_gam = sem("s_gam")
        s_d = sem("s_d")
        s_hi = sem("s_hi")
        s_dfree = sem("s_dfree")
        s_score = sem("s_score")
        s_exp = sem("s_exp")
        s_rest = sem("s_rest")
        s_restp = sem("s_restp")
        s_pfree = sem("s_pfree")
        s_mx = sem("s_mx")
        s_mxf = sem("s_mxf")
        s_oe = sem("s_oe")
        s_rc = sem("s_rc")
        s_pool = sem("s_pool")
        s_post = sem("s_post")
        s_cc = sem("s_cc")
        s_ct = sem("s_ct")
        s_crow = sem("s_crow")
        s_pack = [sem(f"s_pack{i}") for i in range(2)]
        s_qk = sem("s_qk")
        s_sh = sem("s_sh")
        s_g0 = [sem(f"s_g0{i}") for i in range(3)]
        s_gl = sem("s_gl")
        s_gx = sem("s_gx")
        s_gst = sem("s_gst")
        s_gt = sem("s_gt")
        s_gh = sem("s_gh")
        s_gno = sem("s_gno")
        s_rstd = sem("s_rstd")
        s_gv = sem("s_gv")
        s_mark = sem("s_mark")
        s_spmark = sem("s_spmark")
        s_phase = sem("s_phase")
        s_gn0 = sem("s_gn0")
        s_gn = sem("s_gn")
        s_gs = sem("s_gs")
        s_ld = [sem(f"s_ld{i}") for i in range(3)]
        s_add = sem("s_add")
        s_st = [sem(f"s_st{i}") for i in range(3)]

        block = ctx.enter_context(nc.Block())

        class At:

            def __init__(self):
                self.d = self.hi = self.blk = self.gs = self.gn = self.ring = self.qk = self.mxblk = 0

            def goto_body(self, b):
                self.d = self.d + b * (U_GN + U_SC + U_V + BLOCKS * (U_QK + U_FIN))
                self.hi = self.hi + b * (U_V + BLOCKS * U_QK)
                self.blk = self.blk + b * BLOCKS
                self.gs = self.gs + b
                self.gn = self.gn + b
                self.ring = self.ring + b * (BLOCKS + 4)
                self.qk = self.qk + b * BLOCKS
                self.mxblk = self.mxblk + b * BLOCKS
                return self

        def program(eng, do):
            at = At()
            do.open_stats(at)
            do.weights(at)
            do.root(at)
            do.open_norm(at)
            do.qk(at, 0, 0)
            do.qk(at, 0, 1)
            do.opening(at)
            do.shift_parts(at)
            do.qk(at, 1, 0)
            do.shift(at, 0)
            do.qk(at, 1, 1)

            def body(b, at, last):
                for j in range(BLOCKS):
                    following = not last or j + 1 < BLOCKS
                    inside = "" if last else ("", "stats", "norm", "")[j]
                    do.attend(at, b, j, following, inside)
                    if following:
                        do.shift_parts(at)
                    if inside == "norm":
                        do.finish(at, b, j)
                        do.shortcut(at, b + 1)
                    if inside == "stats":
                        do.root(at)
                    if j == BLOCKS - 1 and not last:
                        do.values(at)
                    if not last or j + 2 < BLOCKS:
                        do.qk(at, (j + 2) % BLOCKS, 0)
                    if following:
                        do.shift(at, (j + 1) % 2)
                    if not last or j + 2 < BLOCKS:
                        do.qk(at, (j + 2) % BLOCKS, 1)
                    if inside != "norm":
                        do.finish(at, b, j)

            def placed(b):
                a = At()
                a.d, a.hi, a.blk, a.gs, a.gn = at.d, at.hi, at.blk, at.gs, at.gn
                a.ring, a.qk, a.mxblk = at.ring, at.qk, at.mxblk
                return a.goto_body(b)

            with eng.Fori(0, BATCH - 1) as b:
                body(b, placed(b), False)
            body(BATCH - 1, placed(BATCH - 1), True)

        def pairs(eng, part, chunks):
            lo, hi = Q_PARTS[part]
            if hi - lo == 1:
                chunks(lo, 0)
            else:
                with eng.Fori(lo, hi) as a:
                    chunks(a, lo)

        def attend_chunks(eng, chunk):
            chunk(0, True)
            with eng.Fori(1, NCH) as c:
                chunk(c, False)

        def exps_before(at):
            return at.blk * UNITS

        class Phases:

            def qk_done(self, at, part):
                lo, hi = Q_PARTS[part]
                at.d += 2 * (hi - lo)
                at.hi += 2 * (hi - lo)
                at.qk += part

            def opened(self, at):
                at.d += U_SC + U_V
                at.hi += U_V
                at.ring += CT
                at.mxblk += 1

            def inside(self, at, inside):
                if inside == "stats":
                    at.gs += 1
                if inside == "norm":
                    at.gn += 1

        @block.sync
        def _(sp):
            class Do(Phases):
                def weights(self, at):
                    for i, w in enumerate((wq, wk, wv, wsc)):
                        dst = wnat[i // 2][:, (i % 2) * CT * C:(i % 2 + 1) * CT * C]
                        sp.dma_start(dst.rearrange("p (t c) -> p t c", t=CT),
                                     w.rearrange("(t p) c -> p t c", p=P)).then_inc(s_wld, 16)
                    sp.dma_start(gam[:, :], gamma.partition_broadcast(P)).then_inc(s_gam, 16)

                def pieces(self, b, done, before):
                    rows = x[bass.ds(b * C, C), :].rearrange("(t p) n -> p t n", p=P)
                    with sp.Fori(0, NCH) as c:
                        sp.wait_ge(done, before + c)
                        sp.dma_start(gx[:, :, :], rows[:, :, bass.ds(c * CH, CH)]).then_inc(s_gx, 16)

                def open_stats(self, at):
                    rows = x[0:C, :].rearrange("(t p) n -> p t n", p=P)
                    for c in range(NCH):
                        if c >= 3:
                            sp.wait_ge(s_gst, c - 2)
                        sp.dma_start(gx3[c % 3], rows[:, :, c * CH:(c + 1) * CH]).then_inc(s_g0[c % 3], 16)
                    at.gs += 1

                def open_norm(self, at):
                    rows = x[0:C, :].rearrange("(t p) n -> p t n", p=P)
                    for c in range(NCH):
                        if c < 3:
                            sp.wait_ge(s_gst, NCH - 2 + c)
                        else:
                            sp.wait_ge(s_gl, c - 2)
                        sp.dma_start(gx3[c % 3], rows[:, :, c * CH:(c + 1) * CH]).then_inc(s_g0[c % 3], 16)
                    at.gn += 1

                def stage_packed(self, at):
                    for u in range(2):
                        sp.wait_ge(s_pack[u], PACK * (NCH // 2) * at.qk)
                    sp.sem_inc(s_spmark, 1)

                def stats(self, at, b):
                    self.stage_packed(at)
                    self.pieces(b, s_gst, NCH * at.gs)
                    at.gs += 1

                def norm(self, at, b):
                    self.stage_packed(at)
                    self.pieces(b, s_gno, NCH * (at.gn - 1) + 1)
                    at.gn += 1

                def root(self, at):
                    at.d += U_GN

                def piece(self, at, n):
                    if isinstance(at.ring, int) and at.ring + n // 3 == 0:
                        return
                    sp.wait_ge(s_st[n % 3], 16 * (at.ring + n // 3))

                def shortcut(self, at, b):
                    xv, ov = (t[bass.ds(b * C, C), :].rearrange("(a r p) n -> p a r n", p=P, r=2)
                              for t in (x, out))

                    def load(n):
                        self.piece(at, n)
                        sp.dma_start(xrc[:, n % 3, :].rearrange("p (r n) -> p r n", r=2),
                                     xv[:, n % 2, :, n // 2 * CH:(n // 2 + 1) * CH]).then_inc(s_ld[n % 3], 16)

                    for n in range(3):
                        load(n)
                    for n in range(U_SC):
                        sp.wait_ge(s_add, 3 * at.ring + n + 1)
                        sp.dma_start(ov[:, n % 2, :, n // 2 * CH:(n // 2 + 1) * CH],
                                     xrc[:, n % 3, :].rearrange("p (r n) -> p r n", r=2)
                                     ).then_inc(s_st[n % 3], 16)
                        if n + 3 < U_SC:
                            load(n + 3)
                    at.ring += CT
                    at.d += U_SC

                def opening(self, at):
                    ring = at.ring
                    self.shortcut(at, 0)
                    at.ring, at.d = ring, at.d - U_SC
                    self.opened(at)

                def values(self, at):
                    at.d += U_V
                    at.hi += U_V

                def qk(self, at, j, part):
                    par = j % 2

                    def chunks(a, lo):
                        for u in range(2):
                            q0 = a * PAIR + u * CH
                            sp.wait_ge(s_qk, at.qk * NCH + a * 2 + u + 1)
                            for h in range(2):
                                hp = slice(h * D, (h + 1) * D)
                                for lane, to, parts in ((0, 0, slice(1, 3)),
                                                        (0, 2, slice(1, 4, 2)),
                                                        (D, 0, slice(0, 3, 2))):
                                    sp.dma_start(QK[lane:lane + D, par, h, to:to + 2, bass.ds(q0, CH)],
                                                 stage[hp, u, parts, :]).then_inc(s_pack[u], 16)

                    pairs(sp, part, chunks)
                    self.qk_done(at, part)

                def shift_parts(self, at):
                    pass

                def shift(self, at, par):
                    sp.wait_ge(s_ct, at.mxblk)
                    for h in range(2):
                        for r in range(2):
                            row = (2 * r + h) * MT
                            sp.dma_start(QB[D + r:D + r + 1, par, h, :].rearrange("o (a n) -> o a n", n=P),
                                         cT[row:row + MT, :]).then_inc(s_crow, 16)

                def attend(self, at, b, j, following, inside):
                    for s in range(3):
                        sp.wait_ge(s_st[s], 16 * at.ring)
                    for n in range(3):
                        sp.dma_start(xrc[:, n, :], out[bass.ds(b * C + j * P, P), n * PAIR:(n + 1) * PAIR]
                                     ).then_inc(s_ld[n], 16)
                    if inside == "stats":
                        self.stats(at, b + 1)
                    if inside == "norm":
                        self.norm(at, b + 1)
                    at.blk += 1
                    at.mxblk += 1 if following else 0

                def finish(self, at, b, j):
                    for n in range(3):
                        sp.wait_ge(s_add, 3 * at.ring + n + 1)
                        sp.dma_start(out[bass.ds(b * C + j * P, P), n * PAIR:(n + 1) * PAIR],
                                     xrc[:, n, :]).then_inc(s_st[n], 16)
                    at.ring += 1
                    at.d += U_FIN

            program(sp, Do())
            for s in range(3):
                sp.wait_ge(s_st[s], 16 * BATCH * (CT + BLOCKS))

        @block.tensor
        def _(pe):
            def claim(at, exps=True):
                if exps and not (isinstance(at.blk, int) and at.blk == 0):
                    pe.wait_ge(s_exp, exps_before(at))
                pe.wait_ge(s_dfree, at.d)
                pe.sem_inc(s_phase, 1)

            def three(dst, terms):
                n = 0
                for lhs, rhs in terms:
                    last = pe.matmul(dst, lhs, rhs, start=n == 0, stop=n == len(terms) - 1)
                    n += 1
                return last

            PARTS3 = [(0, 0), (0, 1), (1, 0)]
            xp = (xh, xl)

            class Do(Phases):
                def weights(self, at):
                    pe.wait_ge(s_const, 5)
                    pe.wait_ge(s_wld, 64)
                    for w in range(4):
                        wn = wnat[w // 2][:, (w % 2) * CT * C:(w % 2 + 1) * CT * C].rearrange(
                            "p (t c) -> p t c", t=CT)
                        for t in range(CT):
                            n = w * CT + t
                            if n >= 2:
                                pe.wait_ge(s_dfree, n - 1)
                            for o in range(CT):
                                last = pe.transpose(SL[n % 2][:, 0, o * P:(o + 1) * P],
                                                    wn[:, o, t * P:(t + 1) * P], identf[:, :])
                            last.then_inc(s_d, 1)
                    at.d += U_W
                    at.hi += U_W

                def open_stats(self, at):
                    at.gs += 1

                def root(self, at):
                    claim(at)
                    pe.wait_ge(s_gv, 3 * at.gs - 2)
                    pe.matmul(SL[0][:, 0, 0:CT], gmat[:, :], mv[:, :, 0], start=True, stop=True).then_inc(s_d, 1)
                    pe.wait_ge(s_gv, 3 * at.gs - 1)
                    pe.matmul(SL[1][:, 0, 0:CT], gmat[:, :], gn_var, start=True, stop=True).then_inc(s_d, 1)
                    at.d += U_GN

                def open_norm(self, at):
                    at.gn += 1

                def sum_shortcut(self, at, d, c, n):
                    pe.wait_ge(s_dfree, d - 1)
                    for u in range(2):
                        o0 = (2 * n + u) * P
                        last = three(SL[n][:, u, 0:CH], [
                            (WT[:, 3, wp, t, o0:o0 + P], xp[p][:, t, bass.ds(c * CH, CH)])
                            for t in range(CT) for wp, p in PARTS3])
                    last.then_inc(s_d, 1)

                def sum_values(self, at, d, m, u):
                    pe.wait_ge(s_dfree, d - 1)
                    three(OB[:, u, :], [
                        (xp[p][:, t, bass.ds(m * P, P)], WT[:, 2, wp, t, :])
                        for t in range(CT) for wp, p in PARTS3]).then_inc(s_d, 1)

                def shortcut(self, at, b):
                    pe.wait_ge(s_gno, NCH * (at.gn - 1) + 1)
                    claim(at)
                    with pe.Fori(0, NCH) as c:
                        for n in range(2):
                            self.sum_shortcut(at, at.d + 2 * c + n, c, n)
                    at.ring += CT
                    at.d += U_SC

                def values(self, at):
                    pe.wait_ge(s_oe, NCH * at.blk)
                    claim(at)
                    with pe.Fori(0, MT // 2) as a:
                        for u in range(2):
                            self.sum_values(at, at.d + a * 2 + u, a * 2 + u, u)
                    at.d += U_V
                    at.hi += U_V

                def opening(self, at):
                    for u in range(2):
                        pe.wait_ge(s_pack[u], PACK * (NCH // 2) * at.qk)
                    claim(at)

                    def chunk(c, first):
                        for n in range(5):
                            for k in OPEN_TOPS[n]:
                                self.top(0, c * 2 * MT, c, k, not (first and k < 2))
                            if n < 3:
                                self.sum_values(at, at.d + c * 5 + n, c * 3 + n, n % 2)
                            else:
                                self.sum_shortcut(at, at.d + c * 5 + n, c, n - 3)

                    attend_chunks(pe, chunk)
                    self.opened(at)

                def qk(self, at, j, part):
                    def chunks(a, lo):
                        for u in range(2):
                            pe.wait_ge(s_dfree, at.d + (a - lo) * 2 + u - 1)
                            for w in range(2):
                                last = three(SL[u][:, w, 0:CH], [
                                    (WT[:, w, wp, t, j * P:(j + 1) * P],
                                     xp[p][:, t, bass.ds(a * PAIR + u * CH, CH)])
                                    for t in range(CT) for wp, p in PARTS3])
                            last.then_inc(s_d, 1)

                    if part == 0:
                        if isinstance(at.qk, int) and at.qk == 0:
                            pe.wait_ge(s_gl, NCH)
                        claim(at)
                    pairs(pe, part, chunks)
                    self.qk_done(at, part)

                def top(self, par, n, c, k, wait=True):
                    i, h, t = k // (2 * PARTS), k // PARTS % 2, k % PARTS
                    if wait:
                        pe.wait_ge(s_mxf, n + k - 1)
                    pe.matmul(MX[:, k % 2, 0:CH], QH[:, par, h, bass.ds(c * CH + i * P, P)],
                              KH[:, par, h, t * CH:(t + 1) * CH], start=True, stop=True).then_inc(s_mx, 1)

                def shift_parts(self, at):
                    pass

                def shift(self, at, par):
                    pe.wait_ge(s_cc, 3 * at.mxblk)
                    pe.transpose(MX[0:4 * MT, 0, :].bitcast(F16)[:, 0:P], c16[:, :], identh[:, :]
                                 ).then_inc(s_sh, 1)

                def attend(self, at, b, j, following, inside):
                    par = j % 2
                    for u in range(2):
                        pe.wait_ge(s_pack[u], PACK * (NCH // 2) * at.qk)
                    pe.wait_ge(s_crow, 64 * at.mxblk)
                    claim(at, exps=False)

                    def weigh(q, kk, first=False):
                        pe.wait_ge(s_rest, q * MT + kk + 1)
                        pe.wait_ge(s_restp, q * MT + kk + 1)
                        if kk == 0 and not first:
                            pe.wait_ge(s_oe, q)
                        for h in range(2):
                            v0 = (2 * j + h) * V1
                            for i in range(QT):
                                s0 = h * CH + i * P
                                acc = OB[:, h, i * OW:i * OW + V1]
                                upper = PE32[:, kk % PB, s0:s0 + P].bitcast(BF16)[:, 1:2 * P:2]
                                pe.matmul(acc, upper, V[:, kk, v0:v0 + V1], start=kk == 0 and i == 0,
                                          stop=False, skip_group_check=True)
                                last = pe.matmul(acc[:, D:V1], PLO[:, kk % PB, s0:s0 + P],
                                                 V[:, kk, v0 + D:v0 + V1], start=False,
                                                 stop=kk == MT - 1 and i == QT - 1, skip_group_check=True)
                        last.then_inc(s_pfree, 1)

                    def chunk(c, first):
                        q = at.blk * NCH + c
                        for k in range(MT):
                            if following:
                                self.top(1 - par, (at.mxblk * NCH + c) * 2 * MT, c, 2 * k)
                            if not (first and k < 2):
                                pe.wait_ge(s_exp, q * MT + k - 1)
                            for h in range(2):
                                if following and h:
                                    self.top(1 - par, (at.mxblk * NCH + c) * 2 * MT, c, 2 * k + 1)
                                pe.matmul(SL[k % 2][:, h, 0:CH], KH[:, par, h, k * P:(k + 1) * P],
                                          QH[:, par, h, bass.ds(c * CH, CH)], start=True, stop=False)
                                last = pe.matmul(SL[k % 2][:, h, 0:CH], KB[0:D + 2, par, h, k * P:(k + 1) * P],
                                                 QB[0:D + 2, par, h, bass.ds(c * CH, CH)],
                                                 start=False, stop=True)
                            last.then_inc(s_score, 1)
                            if k >= 2:
                                weigh(q, k - 2, first)
                            elif not first:
                                weigh(q - 1, MT + k - 2)

                    attend_chunks(pe, chunk)
                    for kk in (MT - 2, MT - 1):
                        weigh(at.blk * NCH + NCH - 1, kk)
                    self.inside(at, inside)
                    at.blk += 1
                    at.mxblk += 1 if following else 0

                def finish(self, at, b, j):
                    claim(at)
                    pe.wait_ge(s_post, at.blk * NCH + 1)
                    for n in range(U_FIN):
                        if n >= 2:
                            pe.wait_ge(s_dfree, at.d + n - 1)
                        for u in range(2):
                            for i in range(QT):
                                t = (n * 2 + u) * QT + i
                                last = pe.transpose(SL[n % 2][:, u, i * P:(i + 1) * P],
                                                    attn[:, t * P:(t + 1) * P], identf[:, :])
                        last.then_inc(s_d, 1)
                    at.ring += 1
                    at.d += U_FIN

            program(pe, Do())

        @block.scalar
        def _(act):
            class Do(Phases):
                def weights(self, at):
                    for n in range(U_W):
                        act.wait_ge(s_d, n + 1)
                        act.activation(WT[:, n // CT, 0, n % CT, :], SL[n % 2][:, 0, :], ACT.Copy,
                                       scale=WS).then_inc(s_hi, 1)
                    at.d += U_W
                    at.hi += U_W

                def open_stats(self, at):
                    at.gs += 1

                def root(self, at):
                    act.wait_ge(s_gv, 3 * at.gs)
                    act.activation(gn_root, gn_ve, ACT.Sqrt).then_inc(s_gs, 1)
                    at.d += U_GN

                def norm_piece(self, g, c):
                    act.wait_ge(s_rstd, g + 1)
                    act.wait_ge(s_gx, 16 * (NCH * (2 * g - 1) + c + 1))
                    for t in range(CT):
                        last = act.activation(gx[:, t, :], gx[:, t, :], ACT.Identity,
                                              bias=gn_bias[:, t:t + 1], scale=gn_rstd[:, t:t + 1])
                    last.then_inc(s_gt, 1)
                    act.wait_ge(s_gt, NCH * g + c + 1)
                    act.activation(xh[:, :, bass.ds(c * CH, CH)], gx[:, :, :], ACT.Copy).then_inc(s_gh, 1)

                def open_norm(self, at):
                    for c in range(NCH):
                        act.wait_ge(s_gt, c + 1)
                        act.activation(xh[:, :, c * CH:(c + 1) * CH], gx3[c % 3], ACT.Copy).then_inc(s_gh, 1)
                    at.gn += 1

                def shortcut(self, at, b):
                    at.ring += CT
                    at.d += U_SC

                def take_values(self, d, m, u):
                    act.wait_ge(s_d, d + 1)
                    vv = V[:, bass.ds(m, 1), :].rearrange("p a (h x) -> p (a h) x", x=V1)
                    act.activation(vv[:, :, D:2 * D], OB[:, u, :].rearrange("p (h d) -> p h d", d=D),
                                   ACT.Copy, scale=QS / WS).then_inc(s_hi, 1)

                def values(self, at):
                    with act.Fori(0, MT // 2) as a:
                        for u in range(2):
                            self.take_values(at.d + a * 2 + u, a * 2 + u, u)
                    at.d += U_V
                    at.hi += U_V

                def opening(self, at):
                    with act.Fori(0, NCH) as c:
                        for n in range(3):
                            self.take_values(at.d + c * 5 + n, c * 3 + n, n % 2)
                    self.opened(at)

                def qk(self, at, j, part):
                    def chunks(a, lo):
                        for u in range(2):
                            act.wait_ge(s_d, at.d + (a - lo) * 2 + u + 1)
                            if not (isinstance(a, int) and isinstance(at.qk, int) and a + at.qk == 0):
                                act.wait_ge(s_pack[u], PACK * (NCH // 2 * at.qk + a))
                            act.activation(stage[:, u, 1:3, :], SL[u][:, :, 0:CH],
                                           ACT.Copy, scale=QS / WS).then_inc(s_hi, 1)

                    if part == 0 and isinstance(at.qk, int) and at.qk == 0:
                        act.wait_ge(s_gl, NCH)
                    if part == 0 and not isinstance(at.qk, int):
                        act.wait_ge(s_gno, NCH * (at.gn - 1) + 1)
                        act.wait_ge(s_gst, NCH * at.gs)
                    pairs(act, part, chunks)
                    self.qk_done(at, part)

                def shift_parts(self, at):
                    pass

                def shift(self, at, par):
                    pass

                def attend(self, at, b, j, following, inside):
                    def evacuate(q):
                        act.wait_ge(s_pfree, (q + 1) * MT)
                        act.wait_ge(s_post, q + 1)
                        act.activation(Oe[:, :, :, :],
                                       OB[:, :, 0:QT * OW].rearrange("p h (i x) -> p h i x", x=OW)[:, :, :, 0:V1],
                                       ACT.Copy).then_inc(s_oe, 1)

                    def chunk(c, first):
                        q = at.blk * NCH + c
                        for k in range(MT):
                            if k == 2 and not first:
                                evacuate(q - 1)
                            act.wait_ge(s_score, q * MT + k + 1)
                            if not (first and k < PB):
                                act.wait_ge(s_pfree, q * MT + k - PB + 1)
                            act.activation(PE32[:, k % PB, :].rearrange("p (h n) -> p h n", h=2),
                                           SL[k % 2][:, :, 0:CH], ACT.Exp, scale=1.0 / SS).then_inc(s_exp, 1)
                            if k == 6 and inside == "norm":
                                self.norm_piece(at.gn, c)

                    attend_chunks(act, chunk)
                    evacuate(at.blk * NCH + NCH - 1)
                    self.inside(at, inside)
                    at.blk += 1
                    at.mxblk += 1 if following else 0

                def finish(self, at, b, j):
                    at.ring += 1
                    at.d += U_FIN

            program(act, Do())

        @block.vector
        def _(dve):
            class Do(Phases):
                def weights(self, at):
                    nc.vector.memset(QK[D:D + 2, :, :, 3, :], ONE).then_inc(s_const, 1)
                    nc.vector.memset(V[:, :, :].rearrange("p a (h x) -> p (a h) x", x=V1)[:, :, 2 * D:V1],
                                     1.0).then_inc(s_const, 1)
                    for n in range(U_W):
                        dve.wait_ge(s_hi, n + 1)
                        nc.vector.scalar_tensor_tensor(
                            out=WT[:, n // CT, 1, n % CT, :], in0=SL[n % 2][:, 0, :], scalar=WS,
                            in1=WT[:, n // CT, 0, n % CT, :], op0=ALU.mult, op1=ALU.subtract
                            ).then_inc(s_dfree, 1)
                    dve.wait_ge(s_gam, 16)
                    nc.vector.tensor_scalar(gam[:, :], gam[:, :], 1.0 / QS, None, ALU.mult).then_inc(s_const, 1)
                    at.d += U_W
                    at.hi += U_W

                def stats_piece(self, g, c):
                    dve.wait_ge(s_gx, 16 * (2 * NCH * (g - 1) + c + 1))
                    for t in range(CT):
                        last = nc.vector.bn_stats(stat[:, t, bass.ds(c * 6, 6)], gx[:, t, :])
                    last.then_inc(s_gst, 1)

                def open_stats(self, at):
                    nc.vector.memset(gn[:, :, :], 0.0).then_inc(s_gn0, 1)
                    for c in range(NCH):
                        dve.wait_ge(s_g0[c % 3], 16 * (c // 3 + 1))
                        for t in range(CT):
                            last = nc.vector.bn_stats(stat[:, t, c * 6:c * 6 + 6], gx3[c % 3][:, t, :])
                        last.then_inc(s_gst, 1)
                    dve.wait_ge(s_gn0, 1)
                    at.gs += 1

                def root(self, at):
                    steps = [(at.gs - 1) * 9]

                    def link(ins):
                        steps[0] = steps[0] + 1
                        ins.then_inc(s_gn, 1)
                        dve.wait_ge(s_gn, steps[0])

                    dve.wait_ge(s_gst, NCH * at.gs)
                    nc.vector.tensor_copy(gn_a, gn_b)
                    for t in range(CT):
                        aggr = nc.vector.bn_aggr(mv[:, t, :], stat[:, t, :])
                    aggr.then_inc(s_gv, 1)
                    dve.wait_ge(s_d, at.d + 1)
                    link(nc.vector.tensor_copy(gn_mean, SL[0][:, 0, 0:CT]))
                    link(nc.vector.tensor_tensor(gn_dev, mv[:, :, 0], gn_mean, ALU.subtract))
                    link(nc.vector.tensor_tensor(gn_sq, gn_dev, gn_dev, ALU.mult))
                    nc.vector.tensor_tensor(gn_var, gn_sq, mv[:, :, 1], ALU.add).then_inc(s_gv, 1)
                    dve.wait_ge(s_d, at.d + 2)
                    nc.vector.tensor_scalar(gn_ve, SL[1][:, 0, 0:CT], EPS, None, ALU.add).then_inc(s_gv, 1)
                    dve.wait_ge(s_gs, at.gs)
                    link(nc.vector.reciprocal(gn_r, gn_root))
                    link(nc.vector.tensor_tensor(gn_a, gn_r, gn_r, ALU.mult))
                    link(nc.vector.tensor_tensor(gn_b, gn_a, gn_ve, ALU.mult))
                    link(nc.vector.tensor_scalar(gn_a, gn_b, -0.5, 1.5, ALU.mult, ALU.add))
                    link(nc.vector.tensor_tensor(gn_rstd, gn_r, gn_a, ALU.mult))
                    link(nc.vector.tensor_tensor(gn_b, gn_mean, gn_rstd, ALU.mult))
                    nc.vector.tensor_scalar(gn_bias, gn_b, -1.0, None, ALU.mult).then_inc(s_rstd, 1)
                    dve.wait_ge(s_rstd, at.gs)
                    dve.sem_inc(s_dfree, 2)
                    at.d += U_GN

                def open_norm(self, at):
                    def scale(c):
                        dve.wait_ge(s_g0[c % 3], 16 * (2 + c // 3 + 1))
                        for t in range(CT):
                            last = nc.vector.tensor_scalar(
                                gx3[c % 3][:, t, :], gx3[c % 3][:, t, :], gn_mean[:, t:t + 1],
                                gn_rstd[:, t:t + 1], ALU.subtract, ALU.mult)
                        last.then_inc(s_gt, 1)

                    scale(0)
                    for c in range(NCH):
                        if c + 1 < NCH:
                            scale(c + 1)
                        dve.wait_ge(s_gh, c + 1)
                        nc.vector.tensor_tensor(xl[:, :, c * CH:(c + 1) * CH], gx3[c % 3],
                                                xh[:, :, c * CH:(c + 1) * CH], ALU.subtract).then_inc(s_gl, 1)
                    at.gn += 1

                def add_shortcut(self, d, ring, a, n):
                    dve.wait_ge(s_ld[n % 3], 16 * (ring + a * 2 + n // 3 + 1))
                    dve.wait_ge(s_d, d + 1)
                    piece = xrc[:, n % 3, :].rearrange("p (u n) -> p u n", u=2)
                    nc.vector.scalar_tensor_tensor(
                        out=piece, in0=SL[n % 2][:, :, 0:CH], scalar=1.0 / WS, in1=piece,
                        op0=ALU.mult, op1=ALU.add).then_inc(s_add, 1)
                    dve.wait_ge(s_add, 3 * ring + a * 6 + n + 1)
                    dve.sem_inc(s_dfree, 1)

                def rest_values(self, hi, m, u):
                    dve.wait_ge(s_hi, hi + 1)
                    vv = V[:, bass.ds(m, 1), :].rearrange("p a (h x) -> p (a h) x", x=V1)
                    nc.vector.scalar_tensor_tensor(
                        out=vv[:, :, 0:D], in0=OB[:, u, :].rearrange("p (h d) -> p h d", d=D),
                        scalar=QS / WS, in1=vv[:, :, D:2 * D], op0=ALU.mult, op1=ALU.subtract
                        ).then_inc(s_dfree, 1)

                def shortcut(self, at, b):
                    with dve.Fori(0, 2) as a:
                        for n in range(6):
                            self.add_shortcut(at.d + a * 6 + n, at.ring, a, n)
                    at.ring += CT
                    at.d += U_SC

                def values(self, at):
                    with dve.Fori(0, MT // 2) as a:
                        for u in range(2):
                            self.rest_values(at.hi + a * 2 + u, a * 2 + u, u)
                    at.d += U_V
                    at.hi += U_V

                def opening(self, at):
                    with dve.Fori(0, 2) as a:
                        for e in range(3):
                            c = a * 3 + e
                            for n in range(5):
                                for k in OPEN_TOPS[n]:
                                    self.top(c * 2 * MT, c, k)
                                if n < 3:
                                    self.rest_values(at.hi + c * 3 + n, c * 3 + n, n % 2)
                                else:
                                    self.add_shortcut(at.d + c * 5 + n, at.ring, a, 2 * e + n - 3)
                    self.opened(at)

                def qk(self, at, j, part):
                    def chunks(a, lo):
                        for u in range(2):
                            dve.wait_ge(s_hi, at.hi + (a - lo) * 2 + u + 1)
                            nc.vector.scalar_tensor_tensor(
                                out=stage[:, u, 0:4:3, :], in0=SL[u][:, :, 0:CH], scalar=QS / WS,
                                in1=stage[:, u, 1:3, :], op0=ALU.mult, op1=ALU.subtract).then_inc(s_qk, 1)
                            dve.wait_ge(s_qk, at.qk * NCH + a * 2 + u + 1)
                            dve.sem_inc(s_dfree, 1)

                    pairs(dve, part, chunks)
                    self.qk_done(at, part)

                def top(self, n, c, k):
                    i, h, t = k // (2 * PARTS), k // PARTS % 2, k % PARTS
                    dve.wait_ge(s_mx, n + k + 1)
                    nc.vector.tensor_reduce(mx3[:, h, bass.ds(c * QT * PARTS + i * PARTS + t, 1)],
                                            MX[:, k % 2, 0:CH], AX.X, ALU.max).then_inc(s_mxf, 1)

                def shift_parts(self, at):
                    n = 3 * (at.mxblk - 1)
                    dve.wait_ge(s_mxf, at.mxblk * TOPS)
                    nc.vector.tensor_reduce(cmx[:, :], mx3[:, :, :].rearrange("p h (m t) -> p (h m) t", t=PARTS),
                                            AX.X, ALU.max).then_inc(s_cc, 1)
                    dve.wait_ge(s_cc, n + 1)
                    nc.vector.tensor_scalar(c16[:, 0:2 * MT], cmx[:, :], -1.0 / ONE, None, ALU.mult).then_inc(s_cc, 1)
                    dve.wait_ge(s_cc, n + 2)
                    nc.vector.scalar_tensor_tensor(out=c16[:, 2 * MT:], in0=cmx[:, :], scalar=-1.0 / ONE,
                                                   in1=c16[:, 0:2 * MT], op0=ALU.mult, op1=ALU.subtract
                                                   ).then_inc(s_cc, 1)

                def shift(self, at, par):
                    dve.wait_ge(s_sh, at.mxblk)
                    if not (isinstance(at.mxblk, int) and at.mxblk == 1):
                        dve.wait_ge(s_crow, 64 * (at.mxblk - 1))
                    nc.vector.tensor_copy(cT[:, :], MX[0:4 * MT, 0, :].bitcast(F16)[:, 0:P]).then_inc(s_ct, 1)

                def attend(self, at, b, j, following, inside):
                    def split(q, k):
                        dve.wait_ge(s_exp, q * MT + k + 1)
                        nc.vector.tensor_tensor(
                            PLO[:, k % PB, 0:SHARE], PE32[:, k % PB, 0:SHARE],
                            PE32[:, k % PB, 0:SHARE].bitcast(BF16)[:, 1:2 * SHARE:2],
                            ALU.subtract).then_inc(s_rest, 1)

                    def chunk(c, first):
                        q = at.blk * NCH + c
                        for k in range(MT):
                            if following:
                                self.top((at.mxblk * NCH + c) * 2 * MT, c, 2 * k)
                                self.top((at.mxblk * NCH + c) * 2 * MT, c, 2 * k + 1)
                            if k:
                                split(q, k - 1)
                            elif not first:
                                split(q - 1, MT - 1)
                            if k == 4 and not first:
                                invert(q - 1)
                            if k == 9 and inside == "stats":
                                self.stats_piece(at.gs, c)

                    def invert(q):
                        dve.wait_ge(s_oe, q + 1)
                        nc.vector.reciprocal(rc[:, :, :, :], Oe[:, :, :, 2 * D:V1]).then_inc(s_rc, 1)

                    attend_chunks(dve, chunk)
                    split(at.blk * NCH + NCH - 1, MT - 1)
                    invert(at.blk * NCH + NCH - 1)
                    self.inside(at, inside)
                    at.blk += 1
                    at.mxblk += 1 if following else 0

                def finish(self, at, b, j):
                    for n in range(U_FIN):
                        dve.wait_ge(s_ld[n], 16 * (at.ring + 1))
                        dve.wait_ge(s_d, at.d + n + 1)
                        piece = xrc[:, n, :].rearrange("p (u n) -> p u n", u=2)
                        nc.vector.tensor_tensor(piece, SL[n % 2][:, :, 0:CH], piece, ALU.add).then_inc(s_add, 1)
                        dve.wait_ge(s_add, 3 * at.ring + n + 1)
                        dve.sem_inc(s_dfree, 1)
                    at.ring += 1
                    at.d += U_FIN

            program(dve, Do())

        @block.gpsimd
        def _(pool):
            class Do(Phases):
                def weights(self, at):
                    nc.gpsimd.memset(identf[:, :], 0.0).then_inc(s_pool, 1)
                    nc.gpsimd.memset(identh[:, :], 0.0).then_inc(s_pool, 1)
                    nc.gpsimd.memset(rc[:, :, :, :], 0.0).then_inc(s_post, 1)
                    nc.gpsimd.memset(Oe[:, :, :, :], 0.0).then_inc(s_gno, 1)
                    nc.gpsimd.memset(gmat[:, :], 1.0 / GROUP).then_inc(s_pool, 1)
                    pool.wait_ge(s_pool, 3)
                    for m in (identf, identh):
                        nc.gpsimd.affine_select(out=m[:, :], in_=m[:, :], compare_op=ALU.not_equal, fill=1.0,
                                                base=0, pattern=[[-1, P]], channel_multiplier=1
                                                ).then_inc(s_const, 1)
                    g = gmat[:, :].rearrange("p (g i) -> p g i", i=GROUP)
                    nc.gpsimd.affine_select(out=g, in_=g, compare_op=ALU.is_ge, fill=0.0, base=0,
                                            pattern=[[-GROUP, P // GROUP], [0, GROUP]], channel_multiplier=1
                                            ).then_inc(s_pool, 1)
                    pool.wait_ge(s_pool, 4)
                    nc.gpsimd.affine_select(out=g, in_=g, compare_op=ALU.is_ge, fill=0.0, base=GROUP - 1,
                                            pattern=[[GROUP, P // GROUP], [0, GROUP]], channel_multiplier=-1
                                            ).then_inc(s_const, 1)
                    at.d += U_W
                    at.hi += U_W

                def open_stats(self, at):
                    at.gs += 1

                def root(self, at):
                    at.d += U_GN

                def norm_piece(self, g, c):
                    pool.wait_ge(s_gh, NCH * g + c + 1)
                    pool.sem_inc(s_mark, 1)
                    nc.gpsimd.tensor_tensor(xl[:, :, bass.ds(c * CH, CH)], gx[:, :, :],
                                            xh[:, :, bass.ds(c * CH, CH)], ALU.subtract).then_inc(s_gno, 1)

                def open_norm(self, at):
                    at.gn += 1

                def opening(self, at):
                    self.opened(at)

                def shortcut(self, at, b):
                    at.ring += CT
                    at.d += U_SC

                def values(self, at):
                    at.d += U_V
                    at.hi += U_V

                def qk(self, at, j, part):
                    self.qk_done(at, part)

                def shift_parts(self, at):
                    pass

                def shift(self, at, par):
                    pass

                def attend(self, at, b, j, following, inside):
                    pool.wait_ge(s_d, at.d)

                    def weigh_by(q, c):
                        step = 4 + 2 * q
                        sums = Oe[:, :, :, 0:D]
                        pool.wait_ge(s_oe, q + 1)
                        nc.gpsimd.tensor_tensor(sums, sums, Oe[:, :, :, D:2 * D], ALU.add).then_inc(s_pool, 1)
                        pool.wait_ge(s_rc, q + 1)
                        pool.wait_ge(s_pool, step + 1)
                        nc.gpsimd.tensor_tensor(sums, sums, rc[:, :, :, :].to_broadcast([P, 2, QT, D]),
                                                ALU.mult).then_inc(s_pool, 1)
                        pool.wait_ge(s_pool, step + 2)
                        pool.sem_inc(s_mark, 1)
                        g = gam[:, j * P:(j + 1) * P].rearrange("p (h o d) -> p h o d", h=2, o=1)
                        nc.gpsimd.tensor_tensor(
                            attn[:, bass.ds(c * CH, CH)].rearrange("p (i h d) -> p h i d", h=2, d=D),
                            sums, g.to_broadcast([P, 2, QT, D]), ALU.mult).then_inc(s_post, 1)

                    def chunk(c, first):
                        q = at.blk * NCH + c
                        for k in range(MT):
                            pool.wait_ge(s_exp, q * MT + k + 1)
                            nc.gpsimd.tensor_tensor(
                                PLO[:, k % PB, SHARE:], PE32[:, k % PB, SHARE:],
                                PE32[:, k % PB, SHARE:].bitcast(BF16)[:, 1:2 * (PAIR - SHARE):2],
                                ALU.subtract).then_inc(s_restp, 1)
                            if k == 8 and not first:
                                weigh_by(q - 1, c - 1)
                            if k == 14 and inside == "norm":
                                self.norm_piece(at.gn, c)

                    attend_chunks(pool, chunk)
                    weigh_by(at.blk * NCH + NCH - 1, NCH - 1)
                    self.inside(at, inside)
                    at.blk += 1
                    at.mxblk += 1 if following else 0

                def finish(self, at, b, j):
                    at.ring += 1
                    at.d += U_FIN

            pool.wait_ge(s_gam, 16)
            program(pool, Do())


def kernel(x, L0_conv_Wq, L0_conv_Wk, L0_conv_Wv, L0_conv_Wsc, L0_conv_gamma):
    import numpy as np
    import concourse.bacc as bacc
    from concourse.bass_utils import run_bass_kernel_spmd

    nc = bacc.Bacc("TRN2", target_bir_lowering=False, num_devices=1, dynamic_dma_scratch_size=1024)
    arrays = {
        "x": np.ascontiguousarray(x).reshape(BATCH * C, N),
        "wq": np.ascontiguousarray(L0_conv_Wq),
        "wk": np.ascontiguousarray(L0_conv_Wk),
        "wv": np.ascontiguousarray(L0_conv_Wv),
        "wsc": np.ascontiguousarray(L0_conv_Wsc),
        "gamma": np.ascontiguousarray(L0_conv_gamma).reshape(C),
    }
    args = [nc.dram_tensor(k, a.shape, F32, kind="ExternalInput").ap() for k, a in arrays.items()]
    out = nc.dram_tensor("out", (BATCH * C, N), F32, kind="ExternalOutput").ap()
    build(nc, *args, out)
    r = run_bass_kernel_spmd(nc, [arrays], core_ids=[0])
    return r.results[0]["out"].reshape(np.shape(x))
```

```python
from contextlib import ExitStack

import concourse.bass as bass
from concourse import mybir

F32 = mybir.dt.float32
F16 = mybir.dt.float16
BF16 = mybir.dt.bfloat16
ALU = mybir.AluOpType
ACT = mybir.ActivationFunctionType
AX = mybir.AxisListType

P = 128
BATCH, C, N = 4, 512, 48 * 48
HEADS = 8
D = C // HEADS
CT = C // P
BLOCKS = HEADS // 2
CH = 384
NCH = N // CH
QT = CH // P
MT = N // P
V1 = 2 * D + 1
OW = V1 + 1
PB = 3
PAIR = 2 * CH
PARTS = N // CH
GROUP = C // 32
EPS = 1e-5
WS = 64.0
QS = 8.0
ONE = 256.0
SS = QS * QS
UNITS = NCH * MT
TOPS = 2 * UNITS

HI, HI_KLO, QLO_HI = slice(1, 3), slice(1, 4, 2), slice(0, 3, 2)
PACK_ACT, PACK_DVE, PACK_POOL = (0, 0, 0, HI), (0, 0, 2, HI_KLO), (1, D, 0, QLO_HI)
PACK_FAR = ((0, D, 0, QLO_HI), (1, 0, 0, HI), (1, 0, 2, HI_KLO))
PACK = 3 * 16 + 3
SHARE, SHARE_ALONE = 320, 480
G4 = CT * CH

U_W, U_SC, U_V, U_QK, U_FIN = 4 * CT, CT * 3, MT, NCH, 3
OPEN_TOPS = (range(0, 6), range(6, 12), range(12, 18), range(18, 27), range(27, 36))
LATE = 5
NORM_UNITS = (5, 8, 11, 14)
WEIGH_UNITS = (2, 4, 6)
Q_PARTS = ((0, 1), (1, NCH // 2))


def build(nc, x, wq, wk, wv, wsc, gamma, out):
    ctx = ExitStack()
    with ctx:
        def sb(name, shape, dt):
            return ctx.enter_context(nc.sbuf_tensor(name, shape, dt))

        def sem(name):
            return ctx.enter_context(nc.semaphore(name))

        QK = sb("QK", [P, 2, 2, 4, N], F16)
        QH, KH, QB, KB = (QK[:, :, :, i, :] for i in range(4))
        V = sb("V", [P, MT, HEADS * V1], F16)
        xh = sb("xh", [P, CT, N], F16)
        xl = sb("xl", [P, CT, N], F16)
        WT = sb("WT", [P, 4, 2, CT, C], F16)
        PE32 = sb("PE32", [P, PB, PAIR], F32)
        PLO = sb("PLO", [P, PB, PAIR], F16)
        xr = sb("xr", [P, N], F32)
        gx = sb("gx", [P, CT, CH], F32)
        attn = sb("attn", [P, N], F32)
        Oe = sb("Oe", [P, 2, QT, V1], F32)
        gam = sb("gam", [P, C], F32)
        identf = sb("identf", [P, P], F32)
        identh = sb("identh", [P, P], F16)
        gmat = sb("gmat", [P, P], F32)
        mx3 = sb("mx3", [P, 2, MT * PARTS], F32)
        cmx = sb("cmx", [P, 2 * MT], F32)
        cneg = sb("cneg", [P, 2 * MT], F32)
        c16 = sb("c16", [P, 4 * MT], F16)
        cT = sb("cT", [4 * MT, P], F16)
        rc = sb("rc", [P, 2, QT, 1], F32)
        stat = sb("stat", [P, CT, NCH * 6], F32)
        mv = sb("mv", [P, CT, 2], F32)
        gn = sb("gn", [P, 11, CT], F32)
        gn_mean, gn_dev, gn_sq, gn_var, gn_ve, gn_root, gn_r, gn_a, gn_b, gn_rstd, gn_bias = (
            gn[:, i, :] for i in range(11))

        SL = [ctx.enter_context(nc.psum_tensor(f"SL{i}", [P, 2, 512], F32)) for i in range(2)]
        MX = ctx.enter_context(nc.psum_tensor("MX", [P, 2, 512], F32))
        OB = ctx.enter_context(nc.psum_tensor("OB", [P, 2, 512], F32))

        FIN = (SL[0], MX, OB)
        stage = gx[:, :, :].rearrange("p t n -> p (t n)").bitcast(F16).rearrange(
            "p (s a n) -> p s a n", s=2, a=4)
        gx3 = [t[:, 0:G4].rearrange("p (t n) -> p t n", t=CT) for t in (
            PE32[:, :, :].rearrange("p a n -> p (a n)"), xr, attn)]
        wnat = [t[:, :, :].rearrange("p t n -> p (t n)").bitcast(F32) for t in (xh, xl)]
        xrc = xr[:, :].rearrange("p (s n) -> p s n", s=3)

        s_const = sem("s_const")
        s_wld = [sem(f"s_wld{i}") for i in range(2)]
        s_gam = sem("s_gam")
        s_d = sem("s_d")
        s_hi = sem("s_hi")
        s_dfree = sem("s_dfree")
        s_score = sem("s_score")
        s_exp = sem("s_exp")
        s_rest = sem("s_rest")
        s_restp = sem("s_restp")
        s_pfree = sem("s_pfree")
        s_mx = sem("s_mx")
        s_mxf = sem("s_mxf")
        s_oe = sem("s_oe")
        s_rc = sem("s_rc")
        s_pool = sem("s_pool")
        s_post = sem("s_post")
        s_cc = sem("s_cc")
        s_ct = sem("s_ct")
        s_crow = sem("s_crow")
        s_pack = [sem(f"s_pack{i}") for i in range(2)]
        s_copy = sem("s_copy")
        s_qk = sem("s_qk")
        s_sh = sem("s_sh")
        s_g0 = [sem(f"s_g0{i}") for i in range(3)]
        s_gl = sem("s_gl")
        s_gx = sem("s_gx")
        s_gst = sem("s_gst")
        s_gt = sem("s_gt")
        s_gh = sem("s_gh")
        s_gno = sem("s_gno")
        s_root = sem("s_root")
        s_rstd = sem("s_rstd")
        s_gv = sem("s_gv")
        s_mark = sem("s_mark")
        s_spmark = sem("s_spmark")
        s_phase = sem("s_phase")
        s_gn0 = sem("s_gn0")
        s_gn = sem("s_gn")
        s_gs = sem("s_gs")
        s_ld = [sem(f"s_ld{i}") for i in range(3)]
        s_add = sem("s_add")
        s_st = [sem(f"s_st{i}") for i in range(3)]

        block = ctx.enter_context(nc.Block())

        class At:

            def __init__(self):
                self.d = self.hi = self.blk = self.gs = self.gn = self.ring = self.qk = self.mxblk = 0
                self.finished = False

            def goto_body(self, b):
                self.d = self.d + b * (U_SC + U_V + BLOCKS * (U_QK + U_FIN))
                self.hi = self.hi + b * (U_V + BLOCKS * U_QK)
                self.blk = self.blk + b * BLOCKS
                self.gs = self.gs + b
                self.gn = self.gn + b
                self.ring = self.ring + b * (BLOCKS + 4)
                self.qk = self.qk + b * BLOCKS
                self.mxblk = self.mxblk + b * BLOCKS
                return self

        def program(eng, do):
            at = At()
            for half in range(2):
                do.open_stats(at, half)
                do.weights(at, half)
            do.root(at, 0)
            do.root(at, 1)
            do.open_norm(at)
            do.qk(at, 0, 0)
            do.qk(at, 0, 1)
            do.opening(at)
            do.shift_parts(at)
            do.qk(at, 1, 0)
            do.shift(at, 0)
            do.qk(at, 1, 1)

            def body(b, at, last):
                for j in range(BLOCKS):
                    following = not last or j + 1 < BLOCKS
                    inside = "" if last else ("", "stats", "norm", "")[j]
                    do.attend(at, b, j, following, inside)
                    if following:
                        do.shift_parts(at)
                    if inside == "norm":
                        do.shortcut(at, b + 1)
                    do.so_far(at, b, j)
                    if inside == "stats":
                        do.root(at, 0)
                    if j == BLOCKS - 1 and not last:
                        do.values(at)
                    if not last or j + 2 < BLOCKS:
                        do.qk(at, (j + 2) % BLOCKS, 0)
                    if inside == "stats":
                        do.root(at, 1)
                    if following:
                        do.shift(at, (j + 1) % 2)
                    if not last or j + 2 < BLOCKS:
                        do.qk(at, (j + 2) % BLOCKS, 1)
                    do.finish(at, b, j)

            def placed(b):
                a = At()
                a.d, a.hi, a.blk, a.gs, a.gn = at.d, at.hi, at.blk, at.gs, at.gn
                a.ring, a.qk, a.mxblk = at.ring, at.qk, at.mxblk
                a.finished = at.finished
                return a.goto_body(b)

            with eng.Fori(0, BATCH - 1) as b:
                body(b, placed(b), False)
            body(BATCH - 1, placed(BATCH - 1), True)

        def open_pieces(half):
            return range(half * 3, half * 3 + 3)

        OPEN_NORM = (3, 4, 5, 0, 1, 2)

        def pairs(eng, part, chunks):
            lo, hi = Q_PARTS[part]
            if hi - lo == 1:
                chunks(lo, 0)
            else:
                with eng.Fori(lo, hi) as a:
                    chunks(a, lo)

        def attend_chunks(eng, chunk):
            chunk(0, True)
            with eng.Fori(1, NCH) as c:
                chunk(c, False)

        def tops_at(k, h, first):
            s = 2 * k + h
            if not first:
                return range(s, s + 1)
            ends = [max(0, e - 2 * LATE) * 2 * MT // (2 * MT - 2 * LATE) for e in (s, s + 1)]
            return range(*ends)

        def exps_before(at):
            return at.blk * UNITS

        class Phases:

            def qk_done(self, at, part):
                lo, hi = Q_PARTS[part]
                at.d += 2 * (hi - lo)
                at.hi += 2 * (hi - lo)
                at.qk += part

            def opened(self, at):
                at.d += U_SC + U_V
                at.hi += U_V
                at.ring += CT
                at.mxblk += 1

            def so_far(self, at, b, j):
                pass

            def inside(self, at, inside):
                if inside == "stats":
                    at.gs += 1
                if inside == "norm":
                    at.gn += 1

        @block.sync
        def _(sp):
            class Do(Phases):
                def weights(self, at, half):
                    for i, w in enumerate(((wq, wk), (wv, wsc))[half]):
                        dst = wnat[half][:, i * CT * C:(i + 1) * CT * C]
                        sp.dma_start(dst.rearrange("p (t c) -> p t c", t=CT),
                                     w.rearrange("(t p) c -> p t c", p=P)).then_inc(s_wld[half], 16)
                    if half == 1:
                        sp.dma_start(gam[:, :], gamma.partition_broadcast(P)).then_inc(s_gam, 16)

                def pieces(self, b, done, before):
                    rows = x[bass.ds(b * C, C), :].rearrange("(t p) n -> p t n", p=P)
                    with sp.Fori(0, NCH) as c:
                        sp.wait_ge(done, before + c)
                        sp.dma_start(gx[:, :, :], rows[:, :, bass.ds(c * CH, CH)]).then_inc(s_gx, 16)

                def open_piece(self, c):
                    rows = x[0:C, :].rearrange("(t p) n -> p t n", p=P)
                    sp.dma_start(gx3[c % 3], rows[:, :, c * CH:(c + 1) * CH]).then_inc(s_g0[c % 3], 16)

                def open_stats(self, at, half):
                    for c in open_pieces(half):
                        if c >= 3:
                            sp.wait_ge(s_gst, c - 2)
                        self.open_piece(c)
                    at.gs += half

                def open_norm(self, at):
                    for c in OPEN_NORM[3:]:
                        sp.wait_ge(s_gl, c + 1)
                        self.open_piece(c)
                    at.gn += 1

                def stage_packed(self, at):
                    for u in range(2):
                        sp.wait_ge(s_pack[u], PACK * (NCH // 2) * at.qk)
                    sp.sem_inc(s_spmark, 1)

                def stats(self, at, b):
                    self.stage_packed(at)
                    self.pieces(b, s_gst, NCH * at.gs)
                    at.gs += 1

                def norm(self, at, b):
                    self.stage_packed(at)
                    self.pieces(b, s_gno, NCH * (at.gn - 1) + 1)
                    at.gn += 1

                def root(self, at, part):
                    pass

                def piece(self, at, n):
                    if isinstance(at.ring, int) and at.ring + n // 3 == 0:
                        return
                    sp.wait_ge(s_st[n % 3], 16 * (at.ring + n // 3))

                def shortcut(self, at, b):
                    xv, ov = (t[bass.ds(b * C, C), :].rearrange("(a r p) n -> p a r n", p=P, r=2)
                              for t in (x, out))

                    def load(n):
                        self.piece(at, n)
                        sp.dma_start(xrc[:, n % 3, :].rearrange("p (r n) -> p r n", r=2),
                                     xv[:, n % 2, :, n // 2 * CH:(n // 2 + 1) * CH]).then_inc(s_ld[n % 3], 16)

                    for n in range(3):
                        load(n)
                    for n in range(U_SC):
                        sp.wait_ge(s_add, 3 * at.ring + n + 1)
                        sp.dma_start(ov[:, n % 2, :, n // 2 * CH:(n // 2 + 1) * CH],
                                     xrc[:, n % 3, :].rearrange("p (r n) -> p r n", r=2)
                                     ).then_inc(s_st[n % 3], 16)
                        if n + 3 < U_SC:
                            load(n + 3)
                    at.ring += CT
                    at.d += U_SC

                def opening(self, at):
                    ring = at.ring
                    self.shortcut(at, 0)
                    at.ring, at.d = ring, at.d - U_SC
                    self.opened(at)

                def values(self, at):
                    at.d += U_V
                    at.hi += U_V

                def qk(self, at, j, part):
                    par = j % 2

                    def chunks(a, lo):
                        for u in range(2):
                            q0 = a * PAIR + u * CH
                            sp.wait_ge(s_qk, at.qk * NCH + a * 2 + u + 1)
                            for h, lane, to, parts in PACK_FAR:
                                sp.dma_start(QK[lane:lane + D, par, h, to:to + 2, bass.ds(q0, CH)],
                                             stage[h * D:(h + 1) * D, u, parts, :]).then_inc(s_pack[u], 16)

                    pairs(sp, part, chunks)
                    self.qk_done(at, part)

                def shift_parts(self, at):
                    pass

                def shift(self, at, par):
                    sp.wait_ge(s_ct, at.mxblk)
                    for h in range(2):
                        for r in range(2):
                            row = (2 * r + h) * MT
                            sp.dma_start(QB[D + r:D + r + 1, par, h, :].rearrange("o (a n) -> o a n", n=P),
                                         cT[row:row + MT, :]).then_inc(s_crow, 16)

                def attend(self, at, b, j, following, inside):
                    if inside == "stats":
                        self.stats(at, b + 1)
                    if inside == "norm":
                        self.norm(at, b + 1)
                    at.blk += 1
                    at.mxblk += 1 if following else 0

                def so_far(self, at, b, j):
                    for s in range(3):
                        sp.wait_ge(s_st[s], 16 * at.ring)
                    for n in range(3):
                        sp.dma_start(xrc[:, n, :], out[bass.ds(b * C + j * P, P), n * PAIR:(n + 1) * PAIR]
                                     ).then_inc(s_ld[n], 16)

                def finish(self, at, b, j):
                    for n in range(3):
                        sp.wait_ge(s_add, 3 * at.ring + n + 1)
                        sp.dma_start(out[bass.ds(b * C + j * P, P), n * PAIR:(n + 1) * PAIR],
                                     xrc[:, n, :]).then_inc(s_st[n], 16)
                    at.ring += 1
                    at.d += U_FIN

            program(sp, Do())
            for s in range(3):
                sp.wait_ge(s_st[s], 16 * BATCH * (CT + BLOCKS))

        @block.tensor
        def _(pe):
            def begin(at):
                if not (isinstance(at.blk, int) and at.blk == 0):
                    pe.wait_ge(s_exp, exps_before(at))
                pe.sem_inc(s_phase, 1)

            def three(dst, terms, beside=lambda: None):
                n = 0
                for lhs, rhs in terms:
                    beside()
                    last = pe.matmul(dst, lhs, rhs, start=n == 0, stop=n == len(terms) - 1)
                    n += 1
                return last

            PARTS3 = [(0, 0), (0, 1), (1, 0)]
            xp = (xh, xl)

            class Do(Phases):
                def weights(self, at, half):
                    pe.wait_ge(s_const, 3)
                    pe.wait_ge(s_wld[half], 32)
                    for w in range(2):
                        wn = wnat[half][:, w * CT * C:(w + 1) * CT * C].rearrange("p (t c) -> p t c", t=CT)
                        for t in range(CT):
                            n = (2 * half + w) * CT + t
                            if n >= 2:
                                pe.wait_ge(s_dfree, n - 1)
                            for o in range(CT):
                                last = pe.transpose(SL[n % 2][:, 0, o * P:(o + 1) * P],
                                                    wn[:, o, t * P:(t + 1) * P], identf[:, :])
                            last.then_inc(s_d, 1)
                    at.d += U_W // 2
                    at.hi += U_W // 2

                def open_stats(self, at, half):
                    at.gs += half

                def root(self, at, part):
                    if part == 0:
                        if not (isinstance(at.blk, int) and at.blk == 0):
                            pe.wait_ge(s_oe, NCH * at.blk)
                        pe.wait_ge(s_gv, 3 * at.gs - 2)
                        pe.matmul(OB[:, 0, 0:CT], gmat[:, :], mv[:, :, 0], start=True, stop=True
                                  ).then_inc(s_root, 1)
                    else:
                        pe.wait_ge(s_gv, 3 * at.gs - 1)
                        pe.matmul(OB[:, 1, 0:CT], gmat[:, :], gn_var, start=True, stop=True
                                  ).then_inc(s_root, 1)

                def open_norm(self, at):
                    at.gn += 1

                def sum_shortcut(self, at, d, c, n, beside=lambda: None):
                    pe.wait_ge(s_dfree, d - 1)
                    for u in range(2):
                        o0 = (2 * n + u) * P
                        last = three(SL[n][:, u, 0:CH], [
                            (WT[:, 3, wp, t, o0:o0 + P], xp[p][:, t, bass.ds(c * CH, CH)])
                            for t in range(CT) for wp, p in PARTS3], beside)
                    last.then_inc(s_d, 1)

                def sum_values(self, at, d, m, u, beside=lambda: None):
                    pe.wait_ge(s_dfree, d - 1)
                    three(OB[:, u, :], [
                        (xp[p][:, t, bass.ds(m * P, P)], WT[:, 2, wp, t, :])
                        for t in range(CT) for wp, p in PARTS3], beside).then_inc(s_d, 1)

                def shortcut(self, at, b):
                    pe.wait_ge(s_gno, NCH * (at.gn - 1) + 1)
                    begin(at)
                    with pe.Fori(0, NCH) as c:
                        for n in range(2):
                            self.sum_shortcut(at, at.d + 2 * c + n, c, n)
                    at.ring += CT
                    at.d += U_SC

                def values(self, at):
                    pe.wait_ge(s_oe, NCH * at.blk)
                    begin(at)
                    with pe.Fori(0, MT // 2) as a:
                        for u in range(2):
                            self.sum_values(at, at.d + a * 2 + u, a * 2 + u, u)
                    at.d += U_V
                    at.hi += U_V

                def opening(self, at):
                    for u in range(2):
                        pe.wait_ge(s_pack[u], PACK * (NCH // 2) * at.qk)
                    pe.wait_ge(s_const, 5)
                    begin(at)

                    def chunk(c, first):
                        for n in range(5):
                            todo = list(OPEN_TOPS[n])
                            steps = 3 * CT * (1 if n < 3 else 2)
                            every = steps // len(todo)
                            count = [0]

                            def beside():
                                if count[0] % every == 0 and todo:
                                    k = todo.pop(0)
                                    self.top(0, c * 2 * MT, c, k, not (first and k < 2))
                                count[0] = count[0] + 1

                            if n < 3:
                                self.sum_values(at, at.d + c * 5 + n, c * 3 + n, n % 2, beside)
                            else:
                                self.sum_shortcut(at, at.d + c * 5 + n, c, n - 3, beside)

                    attend_chunks(pe, chunk)
                    self.opened(at)

                def qk(self, at, j, part):
                    def chunks(a, lo):
                        for u in range(2):
                            pe.wait_ge(s_dfree, at.d + (a - lo) * 2 + u - 1)
                            for w in range(2):
                                last = three(SL[u][:, w, 0:CH], [
                                    (WT[:, w, wp, t, j * P:(j + 1) * P],
                                     xp[p][:, t, bass.ds(a * PAIR + u * CH, CH)])
                                    for t in range(CT) for wp, p in PARTS3])
                            last.then_inc(s_d, 1)

                    if part == 0:
                        if isinstance(at.qk, int) and at.qk == 0:
                            pe.wait_ge(s_gl, NCH)
                        begin(at)
                    pairs(pe, part, chunks)
                    self.qk_done(at, part)

                def top(self, par, n, c, k, wait=True):
                    i, h, t = k // (2 * PARTS), k // PARTS % 2, k % PARTS
                    if wait:
                        pe.wait_ge(s_mxf, n + k - 1)
                    pe.matmul(MX[:, k % 2, 0:CH], QH[:, par, h, bass.ds(c * CH + i * P, P)],
                              KH[:, par, h, t * CH:(t + 1) * CH], start=True, stop=True).then_inc(s_mx, 1)

                def shift_parts(self, at):
                    pass

                def shift(self, at, par):
                    pe.wait_ge(s_cc, 3 * at.mxblk)
                    pe.transpose(MX[0:4 * MT, 0, :].bitcast(F16)[:, 0:P], c16[:, :], identh[:, :]
                                 ).then_inc(s_sh, 1)

                def attend(self, at, b, j, following, inside):
                    par = j % 2
                    pe.wait_ge(s_crow, 64 * at.mxblk)

                    def weigh(q, kk, first=False):
                        pe.wait_ge(s_rest, q * MT + kk + 1)
                        pe.wait_ge(s_restp, q * MT + kk + 1)
                        if kk == 0 and first:
                            pe.wait_ge(s_dfree, at.d)
                        if kk == 0 and not first:
                            pe.wait_ge(s_oe, q)
                        for h in range(2):
                            v0 = (2 * j + h) * V1
                            for i in range(QT):
                                s0 = h * CH + i * P
                                acc = OB[:, h, i * OW:i * OW + V1]
                                upper = PE32[:, kk % PB, s0:s0 + P].bitcast(BF16)[:, 1:2 * P:2]
                                pe.matmul(acc, upper, V[:, kk, v0:v0 + V1], start=kk == 0 and i == 0,
                                          stop=False, skip_group_check=True)
                                last = pe.matmul(acc[:, D:V1], PLO[:, kk % PB, s0:s0 + P],
                                                 V[:, kk, v0 + D:v0 + V1], start=False,
                                                 stop=kk == MT - 1 and i == QT - 1, skip_group_check=True)
                        last.then_inc(s_pfree, 1)

                    def chunk(c, first):
                        q = at.blk * NCH + c
                        for k in range(MT):
                            if k == 1 and not first:
                                weigh(q - 1, MT - 1)
                            if k == LATE and first and following:
                                for u in range(2):
                                    pe.wait_ge(s_pack[u], PACK * (NCH // 2) * at.qk)
                            if first and k < 2:
                                pe.wait_ge(s_dfree, at.d - 2 if at.finished else at.d - 1 + k)
                            else:
                                pe.wait_ge(s_exp, q * MT + k - 1)
                            for h in range(2):
                                for n in tops_at(k, h, first) if following else ():
                                    self.top(1 - par, (at.mxblk * NCH + c) * 2 * MT, c, n)
                                pe.matmul(SL[k % 2][:, h, 0:CH], KH[:, par, h, k * P:(k + 1) * P],
                                          QH[:, par, h, bass.ds(c * CH, CH)], start=True, stop=False)
                                last = pe.matmul(SL[k % 2][:, h, 0:CH], KB[0:D + 2, par, h, k * P:(k + 1) * P],
                                                 QB[0:D + 2, par, h, bass.ds(c * CH, CH)],
                                                 start=False, stop=True)
                            last.then_inc(s_score, 1)
                            if k >= 2:
                                weigh(q, k - 2, first)
                            elif k == 0 and not first:
                                weigh(q - 1, MT - 2)

                    attend_chunks(pe, chunk)
                    for kk in (MT - 2, MT - 1):
                        weigh(at.blk * NCH + NCH - 1, kk)
                    at.finished = False
                    self.inside(at, inside)
                    at.blk += 1
                    at.mxblk += 1 if following else 0

                def finish(self, at, b, j):
                    pe.wait_ge(s_post, at.blk * NCH + 1)
                    pe.wait_ge(s_exp, exps_before(at))
                    for n in range(U_FIN):
                        if n == 0:
                            pe.wait_ge(s_dfree, at.d - 1)
                        if n == 1:
                            pe.wait_ge(s_ct, at.mxblk)
                        for u in range(2):
                            for i in range(QT):
                                t = (n * 2 + u) * QT + i
                                last = pe.transpose(FIN[n][:, u, i * P:(i + 1) * P],
                                                    attn[:, t * P:(t + 1) * P], identf[:, :])
                        last.then_inc(s_d, 1)
                    at.ring += 1
                    at.d += U_FIN
                    at.finished = True

            program(pe, Do())

        @block.scalar
        def _(act):
            class Do(Phases):
                def weights(self, at, half):
                    for n in range(half * U_W // 2, (half + 1) * U_W // 2):
                        act.wait_ge(s_d, n + 1)
                        act.activation(WT[:, n // CT, 0, n % CT, :], SL[n % 2][:, 0, :], ACT.Copy,
                                       scale=WS).then_inc(s_hi, 1)
                    at.d += U_W // 2
                    at.hi += U_W // 2

                def open_stats(self, at, half):
                    at.gs += half

                def root(self, at, part):
                    if part == 1:
                        act.wait_ge(s_gv, 3 * at.gs)
                        act.activation(gn_root, gn_ve, ACT.Sqrt).then_inc(s_gs, 1)

                def norm_scale(self, g, c, t):
                    if t == 0:
                        act.wait_ge(s_rstd, g + 1)
                        act.wait_ge(s_gx, 16 * (NCH * (2 * g - 1) + c + 1))
                    act.activation(gx[:, t, :], gx[:, t, :], ACT.Identity, bias=gn_bias[:, t:t + 1],
                                   scale=gn_rstd[:, t:t + 1]).then_inc(s_gt, 1)

                def norm_upper(self, g, c, t):
                    act.wait_ge(s_gt, CT * (NCH * g + c) + t + 1)
                    act.activation(xh[:, t, bass.ds(c * CH, CH)], gx[:, t, :], ACT.Copy).then_inc(s_gh, 1)

                def open_norm(self, at):
                    for n, c in enumerate(OPEN_NORM):
                        act.wait_ge(s_gt, CT * (n + 1))
                        act.activation(xh[:, :, c * CH:(c + 1) * CH], gx3[c % 3], ACT.Copy).then_inc(s_gh, CT)
                    at.gn += 1

                def shortcut(self, at, b):
                    at.ring += CT
                    at.d += U_SC

                def take_values(self, d, m, u):
                    act.wait_ge(s_d, d + 1)
                    vv = V[:, bass.ds(m, 1), :].rearrange("p a (h x) -> p (a h) x", x=V1)
                    act.activation(vv[:, :, D:2 * D], OB[:, u, :].rearrange("p (h d) -> p h d", d=D),
                                   ACT.Copy, scale=QS / WS).then_inc(s_hi, 1)

                def values(self, at):
                    with act.Fori(0, MT // 2) as a:
                        for u in range(2):
                            self.take_values(at.d + a * 2 + u, a * 2 + u, u)
                    at.d += U_V
                    at.hi += U_V

                def opening(self, at):
                    with act.Fori(0, NCH) as c:
                        for n in range(3):
                            self.take_values(at.d + c * 5 + n, c * 3 + n, n % 2)
                    self.opened(at)

                def qk(self, at, j, part):
                    def chunks(a, lo):
                        for u in range(2):
                            act.wait_ge(s_d, at.d + (a - lo) * 2 + u + 1)
                            if not (isinstance(a, int) and isinstance(at.qk, int) and a + at.qk == 0):
                                act.wait_ge(s_pack[u], PACK * (NCH // 2 * at.qk + a))
                            act.activation(stage[:, u, HI, :], SL[u][:, :, 0:CH],
                                           ACT.Copy, scale=QS / WS).then_inc(s_hi, 1)
                            h, lane, to, parts = PACK_ACT
                            act.wait_ge(s_hi, at.hi + (a - lo) * 2 + u + 1)
                            act.activation(QK[lane:lane + D, j % 2, h, to:to + 2, bass.ds(a * PAIR + u * CH, CH)],
                                           stage[lane:lane + D, u, parts, :], ACT.Copy).then_inc(s_pack[u], 1)

                    if part == 0 and not isinstance(at.qk, int):
                        act.wait_ge(s_gno, NCH * (at.gn - 1) + 1)
                        act.wait_ge(s_gst, NCH * at.gs)
                    pairs(act, part, chunks)
                    self.qk_done(at, part)

                def shift_parts(self, at):
                    pass

                def shift(self, at, par):
                    pass

                def attend(self, at, b, j, following, inside):
                    def evacuate(q):
                        act.wait_ge(s_pfree, (q + 1) * MT)
                        act.wait_ge(s_post, q + 1)
                        act.activation(Oe[:, :, :, :],
                                       OB[:, :, 0:QT * OW].rearrange("p h (i x) -> p h i x", x=OW)[:, :, :, 0:V1],
                                       ACT.Copy).then_inc(s_oe, 1)

                    def chunk(c, first):
                        q = at.blk * NCH + c
                        for k in range(MT):
                            if k == 1 and not first:
                                evacuate(q - 1)
                            act.wait_ge(s_score, q * MT + k + 1)
                            if not (first and k < PB):
                                act.wait_ge(s_pfree, q * MT + k - PB + 1)
                            act.activation(PE32[:, k % PB, :].rearrange("p (h n) -> p h n", h=2),
                                           SL[k % 2][:, :, 0:CH], ACT.Exp, scale=1.0 / SS).then_inc(s_exp, 1)
                            if k in NORM_UNITS and inside == "norm":
                                self.norm_scale(at.gn, c, NORM_UNITS.index(k))
                            if k - 1 in NORM_UNITS and inside == "norm":
                                self.norm_upper(at.gn, c, NORM_UNITS.index(k - 1))

                    attend_chunks(act, chunk)
                    evacuate(at.blk * NCH + NCH - 1)
                    self.inside(at, inside)
                    at.blk += 1
                    at.mxblk += 1 if following else 0

                def finish(self, at, b, j):
                    at.ring += 1
                    at.d += U_FIN

            program(act, Do())

        @block.vector
        def _(dve):
            class Do(Phases):
                def weights(self, at, half):
                    for n in range(half * U_W // 2, (half + 1) * U_W // 2):
                        dve.wait_ge(s_hi, n + 1)
                        nc.vector.scalar_tensor_tensor(
                            out=WT[:, n // CT, 1, n % CT, :], in0=SL[n % 2][:, 0, :], scalar=WS,
                            in1=WT[:, n // CT, 0, n % CT, :], op0=ALU.mult, op1=ALU.subtract
                            ).then_inc(s_dfree, 1)
                    at.d += U_W // 2
                    at.hi += U_W // 2

                def stats_piece(self, g, c, t):
                    if t == 0:
                        dve.wait_ge(s_gx, 16 * (2 * NCH * (g - 1) + c + 1))
                    one = nc.vector.bn_stats(stat[:, t, bass.ds(c * 6, 6)], gx[:, t, :])
                    if t == CT - 1:
                        one.then_inc(s_gst, 1)

                def open_stats(self, at, half):
                    if half == 0:
                        nc.vector.memset(gn[:, :, :], 0.0).then_inc(s_gn0, 1)
                    for c in open_pieces(half):
                        dve.wait_ge(s_g0[c % 3], 16 * (c // 3 + 1))
                        for t in range(CT):
                            last = nc.vector.bn_stats(stat[:, t, c * 6:c * 6 + 6], gx3[c % 3][:, t, :])
                        last.then_inc(s_gst, 1)
                    if half == 1:
                        dve.wait_ge(s_gn0, 1)
                    at.gs += half

                def root(self, at, part):
                    steps = [(at.gs - 1) * 9 + 3 * part]

                    def link(ins):
                        steps[0] = steps[0] + 1
                        ins.then_inc(s_gn, 1)
                        dve.wait_ge(s_gn, steps[0])

                    if part == 0:
                        dve.wait_ge(s_gst, NCH * at.gs)
                        nc.vector.tensor_copy(gn_a, gn_b)
                        for t in range(CT):
                            aggr = nc.vector.bn_aggr(mv[:, t, :], stat[:, t, :])
                        aggr.then_inc(s_gv, 1)
                        dve.wait_ge(s_root, 2 * at.gs - 1)
                        link(nc.vector.tensor_copy(gn_mean, OB[:, 0, 0:CT]))
                        link(nc.vector.tensor_tensor(gn_dev, mv[:, :, 0], gn_mean, ALU.subtract))
                        link(nc.vector.tensor_tensor(gn_sq, gn_dev, gn_dev, ALU.mult))
                        nc.vector.tensor_tensor(gn_var, gn_sq, mv[:, :, 1], ALU.add).then_inc(s_gv, 1)
                        return
                    dve.wait_ge(s_root, 2 * at.gs)
                    nc.vector.tensor_scalar(gn_ve, OB[:, 1, 0:CT], EPS, None, ALU.add).then_inc(s_gv, 1)
                    dve.wait_ge(s_gs, at.gs)
                    link(nc.vector.reciprocal(gn_r, gn_root))
                    link(nc.vector.tensor_tensor(gn_a, gn_r, gn_r, ALU.mult))
                    link(nc.vector.tensor_tensor(gn_b, gn_a, gn_ve, ALU.mult))
                    link(nc.vector.tensor_scalar(gn_a, gn_b, -0.5, 1.5, ALU.mult, ALU.add))
                    link(nc.vector.tensor_tensor(gn_rstd, gn_r, gn_a, ALU.mult))
                    link(nc.vector.tensor_tensor(gn_b, gn_mean, gn_rstd, ALU.mult))
                    nc.vector.tensor_scalar(gn_bias, gn_b, -1.0, None, ALU.mult).then_inc(s_rstd, 1)
                    dve.wait_ge(s_rstd, at.gs)

                def open_norm(self, at):
                    def scale(c):
                        dve.wait_ge(s_g0[c % 3], 32 if c >= 3 else 48)
                        for t in range(CT):
                            last = nc.vector.tensor_scalar(
                                gx3[c % 3][:, t, :], gx3[c % 3][:, t, :], gn_mean[:, t:t + 1],
                                gn_rstd[:, t:t + 1], ALU.subtract, ALU.mult)
                        last.then_inc(s_gt, CT)

                    def lower(n):
                        c = OPEN_NORM[n]
                        dve.wait_ge(s_gh, CT * (n + 1))
                        nc.vector.tensor_tensor(xl[:, :, c * CH:(c + 1) * CH], gx3[c % 3],
                                                xh[:, :, c * CH:(c + 1) * CH], ALU.subtract).then_inc(s_gl, 1)

                    scale(OPEN_NORM[0])
                    for n in range(1, NCH):
                        scale(OPEN_NORM[n])
                        lower(n - 1)
                    lower(NCH - 1)
                    dve.wait_ge(s_gam, 16)
                    nc.vector.tensor_scalar(gam[:, :], gam[:, :], 1.0 / QS, None, ALU.mult).then_inc(s_gam, 1)
                    at.gn += 1

                def add_shortcut(self, d, ring, a, n):
                    dve.wait_ge(s_ld[n % 3], 16 * (ring + a * 2 + n // 3 + 1))
                    dve.wait_ge(s_d, d + 1)
                    piece = xrc[:, n % 3, :].rearrange("p (u n) -> p u n", u=2)
                    nc.vector.scalar_tensor_tensor(
                        out=piece, in0=SL[n % 2][:, :, 0:CH], scalar=1.0 / WS, in1=piece,
                        op0=ALU.mult, op1=ALU.add).then_inc(s_add, 1)
                    dve.wait_ge(s_add, 3 * ring + a * 6 + n + 1)
                    dve.sem_inc(s_dfree, 1)

                def rest_values(self, hi, m, u):
                    dve.wait_ge(s_hi, hi + 1)
                    vv = V[:, bass.ds(m, 1), :].rearrange("p a (h x) -> p (a h) x", x=V1)
                    nc.vector.scalar_tensor_tensor(
                        out=vv[:, :, 0:D], in0=OB[:, u, :].rearrange("p (h d) -> p h d", d=D),
                        scalar=QS / WS, in1=vv[:, :, D:2 * D], op0=ALU.mult, op1=ALU.subtract
                        ).then_inc(s_dfree, 1)

                def shortcut(self, at, b):
                    with dve.Fori(0, 2) as a:
                        for n in range(6):
                            self.add_shortcut(at.d + a * 6 + n, at.ring, a, n)
                    at.ring += CT
                    at.d += U_SC

                def values(self, at):
                    with dve.Fori(0, MT // 2) as a:
                        for u in range(2):
                            self.rest_values(at.hi + a * 2 + u, a * 2 + u, u)
                    at.d += U_V
                    at.hi += U_V

                def opening(self, at):
                    with dve.Fori(0, 2) as a:
                        for e in range(3):
                            c = a * 3 + e

                            def use(n):
                                if n < 3:
                                    self.rest_values(at.hi + c * 3 + n, c * 3 + n, n % 2)
                                else:
                                    self.add_shortcut(at.d + c * 5 + n, at.ring, a, 2 * e + n - 3)

                            for n in range(5):
                                for i, k in enumerate(OPEN_TOPS[n]):
                                    if n and i == 2:
                                        use(n - 1)
                                    self.top(c * 2 * MT, c, k)
                            use(4)
                    self.opened(at)

                def qk(self, at, j, part):
                    def chunks(a, lo):
                        for u in range(2):
                            dve.wait_ge(s_hi, at.hi + (a - lo) * 2 + u + 1)
                            nc.vector.scalar_tensor_tensor(
                                out=stage[:, u, 0:4:3, :], in0=SL[u][:, :, 0:CH], scalar=QS / WS,
                                in1=stage[:, u, 1:3, :], op0=ALU.mult, op1=ALU.subtract).then_inc(s_qk, 1)
                            dve.wait_ge(s_qk, at.qk * NCH + a * 2 + u + 1)
                            dve.sem_inc(s_dfree, 1)
                            h, lane, to, parts = PACK_DVE
                            nc.vector.tensor_copy(
                                QK[lane:lane + D, j % 2, h, to:to + 2, bass.ds(a * PAIR + u * CH, CH)],
                                stage[lane:lane + D, u, parts, :]).then_inc(s_pack[u], 1)

                    pairs(dve, part, chunks)
                    self.qk_done(at, part)

                def top(self, n, c, k):
                    i, h, t = k // (2 * PARTS), k // PARTS % 2, k % PARTS
                    dve.wait_ge(s_mx, n + k + 1)
                    nc.vector.tensor_reduce(mx3[:, h, bass.ds(c * QT * PARTS + i * PARTS + t, 1)],
                                            MX[:, k % 2, 0:CH], AX.X, ALU.max).then_inc(s_mxf, 1)

                def shift_parts(self, at):
                    n = 3 * (at.mxblk - 1)
                    dve.wait_ge(s_mxf, at.mxblk * TOPS)
                    nc.vector.tensor_reduce(cmx[:, :], mx3[:, :, :].rearrange("p h (m t) -> p (h m) t", t=PARTS),
                                            AX.X, ALU.max).then_inc(s_cc, 1)
                    dve.wait_ge(s_cc, n + 1)
                    nc.vector.tensor_scalar(c16[:, 0:2 * MT], cmx[:, :], -1.0 / ONE, None, ALU.mult).then_inc(s_cc, 1)
                    dve.wait_ge(s_cc, n + 2)
                    nc.vector.scalar_tensor_tensor(out=c16[:, 2 * MT:], in0=cmx[:, :], scalar=-1.0 / ONE,
                                                   in1=c16[:, 0:2 * MT], op0=ALU.mult, op1=ALU.subtract
                                                   ).then_inc(s_cc, 1)

                def shift(self, at, par):
                    dve.wait_ge(s_sh, at.mxblk)
                    if not (isinstance(at.mxblk, int) and at.mxblk == 1):
                        dve.wait_ge(s_crow, 64 * (at.mxblk - 1))
                    nc.vector.tensor_copy(cT[:, :], MX[0:4 * MT, 0, :].bitcast(F16)[:, 0:P]).then_inc(s_ct, 1)

                def attend(self, at, b, j, following, inside):
                    share = SHARE if following else SHARE_ALONE

                    def split(q, k):
                        dve.wait_ge(s_exp, q * MT + k + 1)
                        nc.vector.tensor_tensor(
                            PLO[:, k % PB, 0:share], PE32[:, k % PB, 0:share],
                            PE32[:, k % PB, 0:share].bitcast(BF16)[:, 1:2 * share:2],
                            ALU.subtract).then_inc(s_rest, 1)

                    def chunk(c, first):
                        q = at.blk * NCH + c
                        for k in range(MT):
                            for h in range(2):
                                for n in tops_at(k, h, first) if following else ():
                                    self.top((at.mxblk * NCH + c) * 2 * MT, c, n)
                                if h == 0 and k:
                                    split(q, k - 1)
                                elif h == 0 and not first:
                                    split(q - 1, MT - 1)
                            if k == 2 and not first:
                                invert(q - 1)
                            if k in NORM_UNITS and inside == "stats":
                                self.stats_piece(at.gs, c, NORM_UNITS.index(k))

                    def invert(q):
                        dve.wait_ge(s_oe, q + 1)
                        nc.vector.reciprocal(rc[:, :, :, :], Oe[:, :, :, 2 * D:V1]).then_inc(s_rc, 1)

                    attend_chunks(dve, chunk)
                    split(at.blk * NCH + NCH - 1, MT - 1)
                    invert(at.blk * NCH + NCH - 1)
                    self.inside(at, inside)
                    at.blk += 1
                    at.mxblk += 1 if following else 0

                def finish(self, at, b, j):
                    for n in range(U_FIN):
                        dve.wait_ge(s_ld[n], 16 * (at.ring + 1))
                        dve.wait_ge(s_d, at.d + n + 1)
                        piece = xrc[:, n, :].rearrange("p (u n) -> p u n", u=2)
                        nc.vector.tensor_tensor(piece, FIN[n][:, :, 0:CH], piece, ALU.add).then_inc(s_add, 1)
                        dve.wait_ge(s_add, 3 * at.ring + n + 1)
                        dve.sem_inc(s_dfree, 1)
                    at.ring += 1
                    at.d += U_FIN

            program(dve, Do())

        @block.gpsimd
        def _(pool):
            class Do(Phases):
                def constants(self):
                    nc.gpsimd.memset(identf[:, :], 0.0).then_inc(s_pool, 1)
                    nc.gpsimd.memset(identh[:, :], 0.0).then_inc(s_pool, 1)
                    nc.gpsimd.memset(rc[:, :, :, :], 0.0).then_inc(s_post, 1)
                    nc.gpsimd.memset(Oe[:, :, :, :], 0.0).then_inc(s_gno, 1)
                    nc.gpsimd.memset(gmat[:, :], 1.0 / GROUP).then_inc(s_pool, 1)
                    pool.wait_ge(s_pool, 3)
                    for m in (identf, identh):
                        nc.gpsimd.affine_select(out=m[:, :], in_=m[:, :], compare_op=ALU.not_equal, fill=1.0,
                                                base=0, pattern=[[-1, P]], channel_multiplier=1
                                                ).then_inc(s_const, 1)
                    g = gmat[:, :].rearrange("p (g i) -> p g i", i=GROUP)
                    nc.gpsimd.affine_select(out=g, in_=g, compare_op=ALU.is_ge, fill=0.0, base=0,
                                            pattern=[[-GROUP, P // GROUP], [0, GROUP]], channel_multiplier=1
                                            ).then_inc(s_pool, 1)
                    pool.wait_ge(s_pool, 4)
                    nc.gpsimd.affine_select(out=g, in_=g, compare_op=ALU.is_ge, fill=0.0, base=GROUP - 1,
                                            pattern=[[GROUP, P // GROUP], [0, GROUP]], channel_multiplier=-1
                                            ).then_inc(s_const, 1)
                    nc.gpsimd.memset(V[:, :, :].rearrange("p a (h x) -> p (a h) x", x=V1)[:, :, 2 * D:V1],
                                     1.0).then_inc(s_const, 1)
                    pool.wait_ge(s_const, 4)
                    nc.gpsimd.memset(QK[D:D + 2, :, :, 3, :], ONE).then_inc(s_const, 1)

                def weights(self, at, half):
                    at.d += U_W // 2
                    at.hi += U_W // 2

                def open_stats(self, at, half):
                    at.gs += half

                def root(self, at, part):
                    pass

                def norm_lower(self, g, c, t):
                    pool.wait_ge(s_gh, CT * (NCH * g + c) + t + 1)
                    pool.sem_inc(s_mark, 1)
                    one = nc.gpsimd.tensor_tensor(xl[:, t, bass.ds(c * CH, CH)], gx[:, t, :],
                                                  xh[:, t, bass.ds(c * CH, CH)], ALU.subtract)
                    if t == CT - 1:
                        one.then_inc(s_gno, 1)

                def open_norm(self, at):
                    at.gn += 1

                def opening(self, at):
                    pool.wait_ge(s_gam, 17)
                    self.opened(at)

                def shortcut(self, at, b):
                    at.ring += CT
                    at.d += U_SC

                def values(self, at):
                    at.d += U_V
                    at.hi += U_V

                def qk(self, at, j, part):
                    h, lane, to, parts = PACK_POOL

                    def chunks(a, lo):
                        for u in range(2):
                            pool.wait_ge(s_qk, at.qk * NCH + a * 2 + u + 1)
                            pool.sem_inc(s_mark, 1)
                            nc.gpsimd.tensor_copy(
                                QK[lane:lane + D, j % 2, h, to:to + 2, bass.ds(a * PAIR + u * CH, CH)],
                                stage[lane:lane + D, u, parts, :]).then_inc(s_copy, 1)
                            pool.wait_ge(s_copy, at.qk * NCH + a * 2 + u + 1)
                            pool.sem_inc(s_pack[u], 1)

                    if part == 0:
                        pool.wait_ge(s_post, at.blk * NCH + 1)
                        pool.sem_inc(s_mark, 1)
                    pairs(pool, part, chunks)
                    self.qk_done(at, part)

                def shift_parts(self, at):
                    pass

                def shift(self, at, par):
                    pass

                def attend(self, at, b, j, following, inside):
                    share = SHARE if following else SHARE_ALONE
                    pool.wait_ge(s_d, at.d)

                    def weigh_by(q, c, step):
                        n = 4 + 2 * q
                        sums = Oe[:, :, :, 0:D]
                        if step == 0:
                            pool.wait_ge(s_oe, q + 1)
                            nc.gpsimd.tensor_tensor(sums, sums, Oe[:, :, :, D:2 * D], ALU.add).then_inc(s_pool, 1)
                            return
                        if step == 1:
                            pool.wait_ge(s_rc, q + 1)
                            pool.wait_ge(s_pool, n + 1)
                            nc.gpsimd.tensor_tensor(sums, sums, rc[:, :, :, :].to_broadcast([P, 2, QT, D]),
                                                    ALU.mult).then_inc(s_pool, 1)
                            return
                        pool.wait_ge(s_pool, n + 2)
                        pool.sem_inc(s_mark, 1)
                        g = gam[:, j * P:(j + 1) * P].rearrange("p (h o d) -> p h o d", h=2, o=1)
                        nc.gpsimd.tensor_tensor(
                            attn[:, bass.ds(c * CH, CH)].rearrange("p (i h d) -> p h i d", h=2, d=D),
                            sums, g.to_broadcast([P, 2, QT, D]), ALU.mult).then_inc(s_post, 1)

                    def chunk(c, first):
                        q = at.blk * NCH + c
                        for k in range(MT):
                            pool.wait_ge(s_exp, q * MT + k + 1)
                            nc.gpsimd.tensor_tensor(
                                PLO[:, k % PB, share:], PE32[:, k % PB, share:],
                                PE32[:, k % PB, share:].bitcast(BF16)[:, 1:2 * (PAIR - share):2],
                                ALU.subtract).then_inc(s_restp, 1)
                            if k in WEIGH_UNITS and not first:
                                weigh_by(q - 1, c - 1, WEIGH_UNITS.index(k))
                            if k - 3 in NORM_UNITS and inside == "norm":
                                self.norm_lower(at.gn, c, NORM_UNITS.index(k - 3))

                    attend_chunks(pool, chunk)
                    for step in range(3):
                        weigh_by(at.blk * NCH + NCH - 1, NCH - 1, step)
                    self.inside(at, inside)
                    at.blk += 1
                    at.mxblk += 1 if following else 0

                def finish(self, at, b, j):
                    at.ring += 1
                    at.d += U_FIN

            do = Do()
            do.constants()
            program(pool, do)


def kernel(x, L0_conv_Wq, L0_conv_Wk, L0_conv_Wv, L0_conv_Wsc, L0_conv_gamma):
    import numpy as np
    import concourse.bacc as bacc
    from concourse.bass_utils import run_bass_kernel_spmd

    nc = bacc.Bacc("TRN2", target_bir_lowering=False, num_devices=1, dynamic_dma_scratch_size=1024)
    arrays = {
        "x": np.ascontiguousarray(x).reshape(BATCH * C, N),
        "wq": np.ascontiguousarray(L0_conv_Wq),
        "wk": np.ascontiguousarray(L0_conv_Wk),
        "wv": np.ascontiguousarray(L0_conv_Wv),
        "wsc": np.ascontiguousarray(L0_conv_Wsc),
        "gamma": np.ascontiguousarray(L0_conv_gamma).reshape(C),
    }
    args = [nc.dram_tensor(k, a.shape, F32, kind="ExternalInput").ap() for k, a in arrays.items()]
    out = nc.dram_tensor("out", (BATCH * C, N), F32, kind="ExternalOutput").ap()
    build(nc, *args, out)
    r = run_bass_kernel_spmd(nc, [arrays], core_ids=[0])
    return r.results[0]["out"].reshape(np.shape(x))
```
